# Optimizing a Trainium2 kernel written in Bass

```python
import numpy as np
import jax
import jax.numpy as jnp

def _softmax(x, axis=-1):
    return jax.nn.softmax(x, axis=axis)

def _gelu(x):
    return jax.nn.gelu(x, approximate=True)

def _silu(x):
    return jax.nn.silu(x)

def _sigmoid(x):
    return jax.nn.sigmoid(x)

def _layernorm(x, axis=-1, eps=1e-05):
    m = jnp.mean(x, axis=axis, keepdims=True)
    v = jnp.var(x, axis=axis, keepdims=True)
    return (x - m) / jnp.sqrt(v + eps)

def _scatter_add(tgt, idx, src, axis=0):
    return tgt.at[idx].add(src)

def _segment_sum(src, seg, n):
    return jax.ops.segment_sum(src, seg, n)
kernel_name = 'mk_adaln_d1_jaxref_r8_275196'

def setup_inputs(seed: int=0):
    np.random.seed(seed)
    _w = jnp.asarray

    def _L0_attn_setup():
        import math
        import jax, jax.numpy as jnp
        import numpy as np
        D_MODEL = 128
        NUM_HEADS = 16
        D_HEAD = D_MODEL // NUM_HEADS
        K_S = 32
        B, N = (2, 256)

        def _attn(x, Wq, bq, Wk, bk, Wv, bv, Wo, bo):
            b, n, _ = x.shape
            q = (x @ Wq.T + bq).reshape(b, n, NUM_HEADS, D_HEAD).transpose(0, 2, 1, 3)
            k = (x @ Wk.T + bk).reshape(b, n, NUM_HEADS, D_HEAD).transpose(0, 2, 1, 3)
            v = (x @ Wv.T + bv).reshape(b, n, NUM_HEADS, D_HEAD).transpose(0, 2, 1, 3)
            scores = jnp.einsum('bhqd,bhkd->bhqk', q, k) / math.sqrt(D_HEAD)
            causal = jnp.triu(jnp.ones((n, n), dtype=bool), k=1)
            neg_inf = jnp.array(-jnp.inf, dtype=scores.dtype)
            scores = jnp.where(causal, neg_inf, scores)
            vals, idx = jax.lax.top_k(scores, K_S)
            masked = jnp.full_like(scores, -jnp.inf)
            masked = jnp.put_along_axis(masked, idx, vals, axis=-1, inplace=False)
            attn = jax.nn.softmax(masked, axis=-1)
            out = jnp.einsum('bhqk,bhkd->bhqd', attn, v)
            out = out.transpose(0, 2, 1, 3).reshape(b, n, D_MODEL)
            y = out @ Wo.T + bo
            return (y, attn.mean(axis=1))

        def _reference_tuple_inner(x, Wq, bq, Wk, bk, Wv, bv, Wo, bo):
            return _attn(x, Wq, bq, Wk, bk, Wv, bv, Wo, bo)
        key = jax.random.key(seed)
        ks = jax.random.split(key, 9)
        s = 1.0 / math.sqrt(D_MODEL)
        return {'x': jax.random.normal(ks[0], (B, N, D_MODEL), dtype=jnp.float32), 'Wq': jax.random.normal(ks[1], (D_MODEL, D_MODEL), dtype=jnp.float32) * s, 'bq': jnp.zeros((D_MODEL,), dtype=jnp.float32), 'Wk': jax.random.normal(ks[2], (D_MODEL, D_MODEL), dtype=jnp.float32) * s, 'bk': jnp.zeros((D_MODEL,), dtype=jnp.float32), 'Wv': jax.random.normal(ks[3], (D_MODEL, D_MODEL), dtype=jnp.float32) * s, 'bv': jnp.zeros((D_MODEL,), dtype=jnp.float32), 'Wo': jax.random.normal(ks[4], (D_MODEL, D_MODEL), dtype=jnp.float32) * s, 'bo': jnp.zeros((D_MODEL,), dtype=jnp.float32)}
    _L0_attn_in = _L0_attn_setup()

    def _L0_ffn_setup():
        import jax, jax.numpy as jnp
        import numpy as np
        from jax import lax
        D = 128
        H = 176
        E = 8
        K = 2
        ROUTER_SCALE = 1.0

        def _expert(x, w1, b1, w3, b3, w2, b2):
            h = jax.nn.silu((x @ w1 + b1) * (x @ w3 + b3))
            return h @ w2 + b2
        key = jax.random.key(seed)
        ks = jax.random.split(key, 16)
        s = 0.02
        inp = {'x': jax.random.normal(ks[0], (2, 256, D), dtype=jnp.float32), 'gate_w': jax.random.normal(ks[1], (E, D), dtype=jnp.float32) * s, 'gate_b': jax.random.normal(ks[2], (E,), dtype=jnp.float32) * s, 'w1': jax.random.normal(ks[3], (E, D, H), dtype=jnp.float32) * s, 'b1': jax.random.normal(ks[4], (E, H), dtype=jnp.float32) * s, 'w3': jax.random.normal(ks[5], (E, D, H), dtype=jnp.float32) * s, 'b3': jax.random.normal(ks[6], (E, H), dtype=jnp.float32) * s, 'w2': jax.random.normal(ks[7], (E, H, D), dtype=jnp.float32) * s, 'b2': jax.random.normal(ks[8], (E, D), dtype=jnp.float32) * s, 'sw1': jax.random.normal(ks[9], (D, H), dtype=jnp.float32) * s, 'sb1': jax.random.normal(ks[10], (H,), dtype=jnp.float32) * s, 'sw3': jax.random.normal(ks[11], (D, H), dtype=jnp.float32) * s, 'sb3': jax.random.normal(ks[12], (H,), dtype=jnp.float32) * s, 'sw2': jax.random.normal(ks[13], (H, D), dtype=jnp.float32) * s, 'sb2': jax.random.normal(ks[14], (D,), dtype=jnp.float32) * s}
        return inp
    _L0_ffn_in = _L0_ffn_setup()
    _L0_c = _w((lambda *s: np.random.randn(*s).astype(np.float32) * 0.05)(8, 128))
    _L0_wmod = _w((lambda *s: np.random.randn(*s).astype(np.float32) * 0.05)(128, 6 * 128) * 128 ** (-0.5))
    _d = {'L0_attn_x': _L0_attn_in['x'], 'L0_attn_Wq': _L0_attn_in['Wq'], 'L0_attn_bq': _L0_attn_in['bq'], 'L0_attn_Wk': _L0_attn_in['Wk'], 'L0_attn_bk': _L0_attn_in['bk'], 'L0_attn_Wv': _L0_attn_in['Wv'], 'L0_attn_bv': _L0_attn_in['bv'], 'L0_attn_Wo': _L0_attn_in['Wo'], 'L0_attn_bo': _L0_attn_in['bo'], 'L0_ffn_gate_w': _L0_ffn_in['gate_w'], 'L0_ffn_gate_b': _L0_ffn_in['gate_b'], 'L0_ffn_w1': _L0_ffn_in['w1'], 'L0_ffn_b1': _L0_ffn_in['b1'], 'L0_ffn_w3': _L0_ffn_in['w3'], 'L0_ffn_b3': _L0_ffn_in['b3'], 'L0_ffn_w2': _L0_ffn_in['w2'], 'L0_ffn_b2': _L0_ffn_in['b2'], 'L0_ffn_sw1': _L0_ffn_in['sw1'], 'L0_ffn_sb1': _L0_ffn_in['sb1'], 'L0_ffn_sw3': _L0_ffn_in['sw3'], 'L0_ffn_sb3': _L0_ffn_in['sb3'], 'L0_ffn_sw2': _L0_ffn_in['sw2'], 'L0_ffn_sb2': _L0_ffn_in['sb2'], 'L0_c': _L0_c, 'L0_wmod': _L0_wmod}
    _x0 = _d['L0_attn_x']
    _d['L0_attn_x'] = jax.random.normal(jax.random.fold_in(jax.random.key(seed), 1), (8, 512, 128), dtype=_x0.dtype)
    del _x0
    return _d

def reference(L0_attn_x, L0_attn_Wq, L0_attn_bq, L0_attn_Wk, L0_attn_bk, L0_attn_Wv, L0_attn_bv, L0_attn_Wo, L0_attn_bo, L0_ffn_gate_w, L0_ffn_gate_b, L0_ffn_w1, L0_ffn_b1, L0_ffn_w3, L0_ffn_b3, L0_ffn_w2, L0_ffn_b2, L0_ffn_sw1, L0_ffn_sb1, L0_ffn_sw3, L0_ffn_sb3, L0_ffn_sw2, L0_ffn_sb2, L0_c, L0_wmod):

    def _L0_attn_ref(x, Wq, bq, Wk, bk, Wv, bv, Wo, bo):
        import math
        import jax, jax.numpy as jnp
        import numpy as np
        D_MODEL = 128
        NUM_HEADS = 16
        D_HEAD = D_MODEL // NUM_HEADS
        K_S = 32
        B, N = (2, 256)

        def _attn(x, Wq, bq, Wk, bk, Wv, bv, Wo, bo):
            b, n, _ = x.shape
            q = (x @ Wq.T + bq).reshape(b, n, NUM_HEADS, D_HEAD).transpose(0, 2, 1, 3)
            k = (x @ Wk.T + bk).reshape(b, n, NUM_HEADS, D_HEAD).transpose(0, 2, 1, 3)
            v = (x @ Wv.T + bv).reshape(b, n, NUM_HEADS, D_HEAD).transpose(0, 2, 1, 3)
            scores = jnp.einsum('bhqd,bhkd->bhqk', q, k) / math.sqrt(D_HEAD)
            causal = jnp.triu(jnp.ones((n, n), dtype=bool), k=1)
            neg_inf = jnp.array(-jnp.inf, dtype=scores.dtype)
            scores = jnp.where(causal, neg_inf, scores)
            vals, idx = jax.lax.top_k(scores, K_S)
            masked = jnp.full_like(scores, -jnp.inf)
            masked = jnp.put_along_axis(masked, idx, vals, axis=-1, inplace=False)
            attn = jax.nn.softmax(masked, axis=-1)
            out = jnp.einsum('bhqk,bhkd->bhqd', attn, v)
            out = out.transpose(0, 2, 1, 3).reshape(b, n, D_MODEL)
            y = out @ Wo.T + bo
            return (y, attn.mean(axis=1))

        def _reference_tuple_inner(x, Wq, bq, Wk, bk, Wv, bv, Wo, bo):
            return _attn(x, Wq, bq, Wk, bk, Wv, bv, Wo, bo)
        return _reference_tuple_inner(x, Wq, bq, Wk, bk, Wv, bv, Wo, bo)[0]

    def _L0_ffn_ref(x, gate_w, gate_b, w1, b1, w3, b3, w2, b2, sw1, sb1, sw3, sb3, sw2, sb2):
        import jax, jax.numpy as jnp
        import numpy as np
        from jax import lax
        D = 128
        H = 176
        E = 8
        K = 2
        ROUTER_SCALE = 1.0

        def _expert(x, w1, b1, w3, b3, w2, b2):
            h = jax.nn.silu((x @ w1 + b1) * (x @ w3 + b3))
            return h @ w2 + b2
        shape = x.shape
        xf = x.reshape(-1, D)
        T = xf.shape[0]
        scores = jax.nn.softmax(xf @ gate_w.T, axis=-1)
        biased = scores + gate_b
        _, idx = lax.top_k(biased, K)
        w = jnp.take_along_axis(scores, idx, axis=-1) * ROUTER_SCALE
        rw = jnp.zeros((T, E), dtype=xf.dtype).at[jnp.arange(T)[:, None], idx].add(w)
        h = jax.nn.silu((jnp.einsum('td,edh->teh', xf, w1) + b1) * (jnp.einsum('td,edh->teh', xf, w3) + b3))
        oe = jnp.einsum('teh,ehd->ted', h, w2) + b2
        y = jnp.einsum('te,ted->td', rw, oe)
        z = _expert(xf, sw1, sb1, sw3, sb3, sw2, sb2)
        return (y + z).reshape(shape)
    x = L0_attn_x
    mod = (_silu(L0_c) @ L0_wmod).reshape(L0_c.shape[0], 6, 1, -1)
    sa, ca, ga, sb, cb, gb = (mod[:, 0], mod[:, 1], mod[:, 2], mod[:, 3], mod[:, 4], mod[:, 5])
    ga = (2 * (ga >= 0) - 1) * jnp.maximum(jnp.abs(ga), 0.25)
    gb = (2 * (gb >= 0) - 1) * jnp.maximum(jnp.abs(gb), 0.25)
    h = _layernorm(x, axis=-1) * (1 + ca) + sa
    x = x + ga * _L0_attn_ref(h, L0_attn_Wq, L0_attn_bq, L0_attn_Wk, L0_attn_bk, L0_attn_Wv, L0_attn_bv, L0_attn_Wo, L0_attn_bo)
    h = _layernorm(x, axis=-1) * (1 + cb) + sb
    x = x + gb * _L0_ffn_ref(h, L0_ffn_gate_w, L0_ffn_gate_b, L0_ffn_w1, L0_ffn_b1, L0_ffn_w3, L0_ffn_b3, L0_ffn_w2, L0_ffn_b2, L0_ffn_sw1, L0_ffn_sb1, L0_ffn_sw3, L0_ffn_sb3, L0_ffn_sw2, L0_ffn_sb2)
    return x

_drawn_inputs = setup_inputs


def setup_inputs(seed=0):
    import zlib

    import numpy as np

    out = dict(_drawn_inputs(seed))
    spreads = {'L0_attn_bq': (0.0, 0.722),
     'L0_attn_bk': (0.0, 2.0),
     'L0_attn_bv': (0.0, 0.344),
     'L0_attn_bo': (0.0, 0.324)}
    factors = {'L0_ffn_gate_w': 8.0,
     'L0_ffn_gate_b': 8.0,
     'L0_ffn_w1': 8.0,
     'L0_ffn_b1': 8.0,
     'L0_ffn_w3': 8.0,
     'L0_ffn_b3': 8.0,
     'L0_ffn_w2': 8.0,
     'L0_ffn_b2': 34.776,
     'L0_ffn_sw1': 8.0,
     'L0_ffn_sb1': 8.0,
     'L0_ffn_sw3': 8.0,
     'L0_ffn_sb3': 8.0,
     'L0_ffn_sw2': 8.0,
     'L0_ffn_sb2': 8.0}
    for name, (base, spread) in spreads.items():
        noise = np.random.default_rng([zlib.crc32(name.encode()), seed]).standard_normal(out[name].shape)
        drawn = base * np.exp(spread * noise) if base else spread * noise
        out[name] = jnp.asarray(drawn.astype(out[name].dtype))
    for name, factor in factors.items():
        out[name] = (out[name] * factor).astype(out[name].dtype)
    return out
```

```python
from contextlib import ExitStack

import concourse.bass as bass
from concourse import mybir

F32 = mybir.dt.float32
BF16 = mybir.dt.bfloat16
U32 = mybir.dt.uint32
ALU = mybir.AluOpType
ACT = mybir.ActivationFunctionType
AX_X = mybir.AxisListType.X

P = 128
B, N, D = 8, 512, 128
NH, DH, TOP = 16, 8, 32
NQ = N // P
E, HID = 8, 176
FT = -(-(E + 1) * HID // P)
SCALE = DH ** -0.5
EPS = 1e-5
MASKED = -1e30
TAKEN = -1e38

TILES = ((3, 0), (2, 512), (0, 896), (1, 1024))
COLS = sum(P * (q + 1) for q, _ in TILES)
CHUNK_OF = (0, 1, 1, 2)
CHUNKS = ((0, 512), (512, 1024), (1024, 1280))
NC_ = len(CHUNKS)
SEARCH = 2 * 4 * len(TILES)
ROUTE = 13
FIRST_FFN_HEAD = NH - FT


def after(eng, sem, value):
    if isinstance(value, int) and value <= 0:
        return
    eng.wait_ge(sem, value)


def apart(eng, sem, value):
    after(eng, sem, value)
    if not isinstance(value, int):
        eng.nop(nofuse=True)


def build_program(nc, x_d, weights, out_d):
    ctx = ExitStack()
    with ctx:
        def sb(name, shape, dt=F32):
            return ctx.enter_context(nc.sbuf_tensor(name, shape, dt))

        def ps(name, shape):
            return ctx.enter_context(nc.psum_tensor(name, shape, F32))

        def sem(name):
            return ctx.enter_context(nc.semaphore(name))

        W = {}
        for name, ap in weights.items():
            W[name] = sb("w_" + name, list(ap.shape))
        ident = W["ident"]
        identb = sb("identb", [P, P], BF16)
        cmaskb = sb("cmaskb", [P, P], BF16)
        c_tanh = sb("c_tanh", [P, B])
        c_half = sb("c_half", [P, B])
        c_silu = sb("c_silu", [P, B])
        mod = sb("mod", [P, 6, B])
        g_sign = sb("g_sign", [P, 2, B])
        g_neg = sb("g_neg", [P, 2, B])
        bq_m = sb("bq_m", [P, 4])
        bo_all = sb("bo_all", [P, 1])
        ga_bo = sb("ga_bo", [P, B])
        minus_half = sb("minus_half", [P, NQ])

        xin = sb("xin", [P, NQ, D])
        xres = sb("xres", [P, NQ, D])
        stats = sb("stats", [P, 2, NQ, 6])
        meanvar = sb("meanvar", [P, 2, NQ, 2])
        veps = sb("veps", [P, 2, NQ])
        rstd = sb("rstd", [P, 2, NQ])
        mrs = sb("mrs", [P, 2, NQ])
        nmr = sb("nmr", [P, 2, NQ])
        xn1 = sb("xn1", [P, NQ, D])
        xn2 = sb("xn2", [P, NQ, D])
        hT = sb("hT", [P, N])
        KT = sb("KT", [P, N])
        QT = sb("QT", [P, 4, N])
        VX = sb("VX", [P, NQ, NH, DH + 1])
        S = sb("S", [P, 2, COLS])
        WORK = sb("WORK", [P, 2, COLS])
        TOPV = sb("TOPV", [P, 2, NQ, TOP])
        NMAX = sb("NMAX", [P, 2, NQ])
        E1 = sb("E1", [P, 2, COLS])
        E2 = sb("E2", [P, 2, COLS])
        PT = sb("PT", [P, COLS])
        rsum = sb("rsum", [P, NQ, NH])
        osb = sb("osb", [P, NQ, NH, DH])
        OT = sb("OT", [P, N])
        yT = sb("yT", [P, N])
        x2 = sb("x2", [P, NQ, D])

        h2T = sb("h2T", [P, N])
        rmax = sb("rmax", [P, NQ])
        rdif = sb("rdif", [P, NQ, E])
        rexp = sb("rexp", [P, NQ, E])
        rs = sb("rs", [P, NQ])
        rinv = sb("rinv", [P, NQ])
        rscore = sb("rscore", [P, NQ, E])
        rbias = sb("rbias", [P, NQ, E])
        rtop = sb("rtop", [P, NQ, 8])
        ridx = sb("ridx", [P, NQ, 8], U32)
        ridf = sb("ridf", [P, NQ, 2])
        rhit = sb("rhit", [P, 2, NQ, E])
        rw = sb("rw", [P, NQ, P])
        rwT = sb("rwT", [E + 1, N])
        fa = sb("fa", [P, 2, N])
        fc = sb("fc", [P, 2, N])
        fu = sb("fu", [P, 2, N])
        ft = sb("ft", [P, 2, N])
        ft1 = sb("ft1", [P, 2, N])
        fr = sb("fr", [P, 2, N])
        fv = sb("fv", [P, 2, N])
        fh = sb("fh", [P, 2, N])
        zT = sb("zT", [P, N])
        osum = sb("osum", [P, NQ, D])

        pS = ps("pS", [P, NC_ * 512])
        pT = ps("pT", [P, 512])
        F0 = ps("F0", [P, 512])
        F1 = ps("F1", [P, 512])
        pY = ps("pY", [P, 512])
        pO = ps("pO", [P, 512])
        WO = NH * (DH + 1)
        o_at = {3: pO[:, 0:WO], 2: pO[:, WO:2 * WO], 1: pO[:, 2 * WO:3 * WO], 0: pS[:, COLS:COLS + WO]}

        names = """w_loaded ffn_loaded xin_loaded xres_loaded stored
            const_ready vx_ones rw_ready setup_act setup_dve setup_pe
            scores scopied nmax_done e1_done e2_done search p_done pt_full pt_evac pv_done
            kq_full k_evac q_evac v_full v_evac
            bn1 rstd1 ln1_done ln1T_full hT_done
            norm_done OT_full OT_evac wo_full yT_done att_full res_done bn2 rstd2 ln2_done ln2T_full h2T_done
            log_full rsub_done rexp_done route rw_done rwT_full rwT_done
            up1_full up3_full gate_full a_done c_done u_done t_done t1_done r_done v_done h_done w2_done
            y_full z_done zT_full fin_done norm_step sub_step pool_step1_in pool_step1 pool_step2"""
        s = {n: sem("s_" + n) for n in names.split()}

        ffn_names = ("w1", "w3", "w2", "sel", "b1", "b3", "b2", "gwT", "gb", "iota")
        block = ctx.enter_context(nc.Block())

        def xrows(d, b):
            return d[bass.ds(b, 1), :, :].rearrange("o (q p) d -> p (o q) d", p=P)

        @block.sync
        def _(sp):
            def load_x(b):
                after(sp, s["ln1_done"], b)
                sp.dma_start(xin[:, :, :], xrows(x_d, b)).then_inc(s["xin_loaded"], 16)

            def load_xres(b):
                after(sp, s["res_done"], b)
                sp.dma_start(xres[:, :, :], xrows(x_d, b)).then_inc(s["xres_loaded"], 16)

            def store(b):
                sp.wait_ge(s["fin_done"], b + 1)
                sp.dma_start(xrows(out_d, b), osum[:, :, :]).then_inc(s["stored"], 16)

            load_x(0)
            for name in weights:
                if name not in ffn_names:
                    sp.dma_start(W[name][:, :], weights[name]).then_inc(s["w_loaded"], 16)
            for name in ffn_names:
                sp.dma_start(W[name][:, :], weights[name]).then_inc(s["ffn_loaded"], 16)
            load_xres(0)
            load_x(1)
            with sp.Fori(1, B - 1) as b:
                load_x(b + 1)
                load_xres(b)
                sp.wait_ge(s["fin_done"], b)
                sp.dma_start(xrows(out_d, b - 1), osum[:, :, :]).then_inc(s["stored"], 16)
            load_xres(B - 1)
            store(B - 2)
            store(B - 1)
            sp.wait_ge(s["stored"], 16 * B)

        n_attn_loads = 16 * (len(weights) - len(ffn_names))
        n_ffn_loads = 16 * len(ffn_names)

        @block.gpsimd
        def _(pool):
            pool.memset(minus_half[:, :], -0.5).then_inc(s["const_ready"], 1)
            pool.memset(VX[:, :, :, :], 1.0).then_inc(s["vx_ones"], 1)
            pool.memset(rw[:, :, :], 0.0).then_inc(s["rw_ready"], 1)
            pool.wait_ge(s["rw_ready"], 1)
            pool.memset(rw[:, :, E:E + 1], 1.0).then_inc(s["rw_ready"], 1)
            pool.wait_ge(s["w_loaded"], n_attn_loads)
            pool.tensor_copy(identb[:, :], ident[:, :]).then_inc(s["const_ready"], 1)
            pool.tensor_copy(cmaskb[:, :], W["cmask"][:, :]).then_inc(s["const_ready"], 1)

            def rsqrt(ln, bb, bn, step, done):
                apart(pool, s[bn], bb + 1)
                pool.tensor_scalar(veps[:, ln, :], meanvar[:, ln, :, 1], EPS, 1.0, ALU.add, ALU.mult).then_inc(s[step], 1)
                pool.wait_ge(s[step], 3 * bb + 1)
                pool.tensor_tensor(rstd[:, ln, :], veps[:, ln, :], minus_half[:, :], ALU.pow).then_inc(s[step], 1)
                pool.wait_ge(s[step], 3 * bb + 2)
                pool.tensor_tensor(mrs[:, ln, :], meanvar[:, ln, :, 0], rstd[:, ln, :], ALU.mult).then_inc(s[step], 1)
                apart(pool, s[step], 3 * bb + 3)
                pool.tensor_scalar(nmr[:, ln, :], mrs[:, ln, :], -1.0, 1.0, ALU.mult, ALU.mult).then_inc(s[done], 1)

            def neg_max(H, par):
                apart(pool, s["search"], SEARCH * H + len(TILES))
                pool.tensor_scalar(NMAX[:, par, :], TOPV[:, par, :, 0], -SCALE, 1.0, ALU.mult,
                                   ALU.mult).then_inc(s["nmax_done"], 1)

            def keep_selected(H, par):
                for k, (q, at) in enumerate(TILES):
                    n = P * (q + 1)
                    pool.wait_ge(s["e2_done"], 4 * H + k + 1)
                    pool.tensor_tensor(E1[:, par, at:at + n], E1[:, par, at:at + n], E2[:, par, at:at + n],
                                       ALU.subtract).then_inc(s["p_done"], 1)

            def gate_product(T, tp):
                pool.wait_ge(s["c_done"], T + 1)
                pool.tensor_tensor(fu[:, tp, :], fa[:, tp, :], fc[:, tp, :], ALU.mult).then_inc(s["u_done"], 1)
                apart(pool, s["t_done"], T + 1)
                pool.tensor_scalar(ft1[:, tp, :], ft[:, tp, :], 1.0, 1.0, ALU.add, ALU.mult).then_inc(s["t1_done"], 1)

            def weigh(T, tp):
                pool.wait_ge(s["r_done"], T + 1)
                pool.tensor_tensor(fv[:, tp, :], fu[:, tp, :], fr[:, tp, :], ALU.mult).then_inc(s["v_done"], 1)
                pool.wait_ge(s["v_done"], T + 1)
                pool.tensor_tensor(fh[:, tp, :], fv[:, tp, :], ft1[:, tp, :], ALU.mult).then_inc(s["h_done"], 1)

            def head(b, h, ffn, par):
                H = NH * b + h
                neg_max(H, par)
                if ffn:
                    T = FT * (b - 1) + h - FIRST_FFN_HEAD
                    tp = (par + FIRST_FFN_HEAD) % 2
                    gate_product(T, tp)
                    weigh(T, tp)
                keep_selected(H, par)

            def batch(b, prep, ffn):
                head(b, 0, False, 0)
                head(b, 1, False, 1)
                if ffn:
                    rsqrt(1, b - 1, "bn2", "pool_step2", "rstd2")
                if prep:
                    rsqrt(0, b + 1, "bn1", "pool_step1", "rstd1")
                head(b, 2, False, 0)
                neg_max(NH * b + 3, 1)
                if ffn:
                    gate_product(FT * (b - 1), 0)
                keep_selected(NH * b + 3, 1)
                if ffn:
                    weigh(FT * (b - 1), 0)
                with pool.Fori(2, NH // 2) as p:
                    head(b, 2 * p, ffn, 0)
                    head(b, 2 * p + 1, ffn, 1)

            rsqrt(0, 0, "bn1", "pool_step1", "rstd1")
            batch(0, True, False)
            with pool.Fori(1, B - 1) as b:
                batch(b, True, True)
            batch(B - 1, False, True)
            rsqrt(1, B - 1, "bn2", "pool_step2", "rstd2")
            gate_product(FT * (B - 1), 0)
            weigh(FT * (B - 1), 0)
            with pool.Fori(0, (FT - 1) // 2) as i:
                for j in range(2):
                    T = FT * (B - 1) + 1 + 2 * i + j
                    gate_product(T, 1 - j)
                    weigh(T, 1 - j)

        @block.vector
        def _(dve):
            def head(b, h, par):
                H = NH * b + h
                for r in range(TOP // 8):
                    for k, (q, at) in enumerate(TILES):
                        n = P * (q + 1)
                        src = (WORK if r else S)[:, par, at:at + n]
                        if r == 0:
                            if k == 0:
                                apart(dve, s["nmax_done"], H - 1)
                            apart(dve, s["scopied"], NC_ * H + CHUNK_OF[k] + 1)
                        else:
                            apart(dve, s["search"], SEARCH * H + 8 * r - 4 + k + 1)
                        dve.max(TOPV[:, par, q, 8 * r:8 * r + 8], src).then_inc(s["search"], 1)
                    for k, (q, at) in enumerate(TILES):
                        n = P * (q + 1)
                        src = (WORK if r else S)[:, par, at:at + n]
                        if r == 0:
                            apart(dve, s["e2_done"], 4 * (H - 2) + k + 1)
                        apart(dve, s["search"], SEARCH * H + 8 * r + k + 1)
                        dve.match_replace(out=WORK[:, par, at:at + n], in_to_replace=TOPV[:, par, q, 8 * r:8 * r + 8],
                                          in_values=src, imm_value=TAKEN).then_inc(s["search"], 1)

            def statistics(ln, src, bb, step, done):
                for q in range(NQ):
                    dve.bn_stats(stats[:, ln, q, :], src[:, q, :]).then_inc(s[step], 1)
                for q in range(NQ):
                    apart(dve, s[step], 4 * bb + q + 1)
                    last = dve.bn_aggr(meanvar[:, ln, q, :], stats[:, ln, q, :])
                last.then_inc(s[done], 1)

            def normalise_heads(b, prev_scores):
                dve.wait_ge(s["pv_done"], NH * (b + 1))
                if prev_scores is not None:
                    dve.wait_ge(s["scopied"], prev_scores)
                big = pO[:, 0:3 * WO].rearrange("p (q h c) -> p q h c", q=3, c=DH + 1)
                small = pS[:, COLS:COLS + WO].rearrange("p (h c) -> p h c", c=DH + 1)
                dve.reciprocal(rsum[:, 1:4, :], big[:, :, :, DH]).then_inc(s["norm_step"], 1)
                dve.reciprocal(rsum[:, 0, :], small[:, :, DH]).then_inc(s["norm_step"], 1)
                after(dve, s["OT_full"], b)
                dve.wait_ge(s["norm_step"], 2 * b + 1)
                for i, q in enumerate((3, 2, 1)):
                    dve.tensor_tensor(osb[:, q, :, :], big[:, i, :, 0:DH],
                                      rsum[:, 1 + i, :].unsqueeze(2).to_broadcast([P, NH, DH]), ALU.mult)
                dve.wait_ge(s["norm_step"], 2 * b + 2)
                dve.tensor_tensor(osb[:, 0, :, :], small[:, :, 0:DH],
                                  rsum[:, 0, :].unsqueeze(2).to_broadcast([P, NH, DH]),
                                  ALU.mult).then_inc(s["norm_done"], 1)

            def finish(fb):
                dve.wait_ge(s["zT_full"], fb + 1)
                after(dve, s["stored"], 16 * fb)
                dve.tensor_tensor(osum[:, :, :], x2[:, :, :], F1[:, :].rearrange("p (q d) -> p q d", q=NQ),
                                  ALU.add).then_inc(s["fin_done"], 1)

            def residual(b):
                dve.wait_ge(s["att_full"], b + 1)
                dve.wait_ge(s["xres_loaded"], 16 * (b + 1))
                dve.tensor_tensor(x2[:, :, :], xres[:, :, :], F0[:, :].rearrange("p (q d) -> p q d", q=NQ),
                                  ALU.add).then_inc(s["res_done"], 1)
                apart(dve, s["res_done"], b + 1)
                statistics(1, x2, b, "sub_step", "bn2")

            def logits_minus_max(b):
                logits = F1[:, 0:NQ * E].rearrange("p (q e) -> p q e", q=NQ)
                dve.wait_ge(s["log_full"], b + 1)
                dve.tensor_reduce(rmax[:, :], logits, AX_X, ALU.max).then_inc(s["route"], 1)
                dve.wait_ge(s["route"], ROUTE * b + 1)
                dve.tensor_tensor(rdif[:, :, :], logits, rmax[:, :].unsqueeze(2).to_broadcast([P, NQ, E]),
                                  ALU.subtract).then_inc(s["rsub_done"], 1)

            def routing(b):
                at = [ROUTE * b + 1]

                def step(ins):
                    ins.then_inc(s["route"], 1)
                    at[0] = at[0] + 1

                def settle():
                    apart(dve, s["route"], at[0])

                dve.wait_ge(s["rexp_done"], b + 1)
                dve.wait_ge(s["ffn_loaded"], n_ffn_loads)
                step(dve.tensor_reduce(rs[:, :], rexp[:, :, :], AX_X, ALU.add))
                settle()
                step(dve.reciprocal(rinv[:, :], rs[:, :]))
                settle()
                step(dve.tensor_tensor(rscore[:, :, :], rexp[:, :, :],
                                       rinv[:, :].unsqueeze(2).to_broadcast([P, NQ, E]), ALU.mult))
                settle()
                step(dve.tensor_tensor(rbias[:, :, :], rscore[:, :, :],
                                       W["gb"][:, :].unsqueeze(1).to_broadcast([P, NQ, E]), ALU.add))
                settle()
                for q in range(NQ):
                    ins = dve.max(rtop[:, q, :], rbias[:, q, :])
                step(ins)
                settle()
                for q in range(NQ):
                    ins = dve.max_index(ridx[:, q, :], rtop[:, q, :], rbias[:, q, :])
                step(ins)
                settle()
                step(dve.tensor_copy(ridf[:, :, :], ridx[:, :, 0:2]))
                settle()
                for i in range(2):
                    step(dve.tensor_tensor(rhit[:, i, :, :], ridf[:, :, i:i + 1].to_broadcast([P, NQ, E]),
                                           W["iota"][:, :].unsqueeze(1).to_broadcast([P, NQ, E]), ALU.is_equal))
                settle()
                step(dve.tensor_tensor(rhit[:, 0, :, :], rhit[:, 0, :, :], rhit[:, 1, :, :], ALU.add))
                settle()
                step(dve.tensor_tensor(rdif[:, :, :], rhit[:, 0, :, :], rscore[:, :, :], ALU.mult))
                settle()
                after(dve, s["rwT_full"], b)
                step(dve.tensor_copy(rw[:, :, 0:E], rdif[:, :, :]))
                settle()
                dve.tensor_copy(rw[:, :, 0:E], rdif[:, :, :]).then_inc(s["rw_done"], 1)

            def batch(b, prep, ffn, old):
                head(b, 0, 0)
                if old:
                    finish(b - 2)
                if ffn:
                    normalise_heads(b - 1, NC_ * (NH * b + 1) + NC_)
                head(b, 1, 1)
                if ffn:
                    residual(b - 1)
                if prep:
                    dve.wait_ge(s["xin_loaded"], 16 * (b + 2))
                    statistics(0, xin, b + 1, "pool_step1_in", "bn1")
                head(b, 2, 0)
                if ffn:
                    logits_minus_max(b - 1)
                head(b, 3, 1)
                if ffn:
                    routing(b - 1)
                with dve.Fori(2, NH // 2) as p:
                    head(b, 2 * p, 0)
                    head(b, 2 * p + 1, 1)

            at = [0]

            def link(ins):
                at[0] += 1
                ins.then_inc(s["setup_dve"], 1)
                dve.wait_ge(s["setup_dve"], at[0])

            dve.wait_ge(s["xin_loaded"], 16)
            statistics(0, xin, 0, "pool_step1_in", "bn1")
            dve.wait_ge(s["setup_act"], 1)
            link(dve.tensor_scalar(c_half[:, :], W["cT"][:, :], 0.5, None, ALU.mult))
            link(dve.scalar_tensor_tensor(out=c_silu[:, :], in0=c_tanh[:, :], scalar=1.0, in1=c_half[:, :],
                                          op0=ALU.add, op1=ALU.mult))
            for j in range(4):
                ins = dve.tensor_tensor(bq_m[:, j:j + 1], W["bq"][:, :], W["hmask"][:, j:j + 1], ALU.mult)
            link(ins)
            dve.wait_ge(s["setup_pe"], 1)
            link(dve.tensor_copy(mod[:, :, :], F0[:, 0:6 * B].rearrange("p (m b) -> p m b", m=6)))
            link(dve.tensor_tensor(bo_all[:, :], W["bo"][:, :], F0[:, 6 * B:6 * B + 1], ALU.add))
            for i in (1, 4):
                link(dve.tensor_scalar(mod[:, i, :], mod[:, i, :], 1.0, None, ALU.add))
            for i, m in enumerate((2, 5)):
                link(dve.tensor_scalar(g_sign[:, i, :], mod[:, m, :], 0.0, 2.0, ALU.is_ge, ALU.mult))
                link(dve.tensor_scalar(g_sign[:, i, :], g_sign[:, i, :], -1.0, None, ALU.add))
                link(dve.tensor_scalar(g_neg[:, i, :], mod[:, m, :], -1.0, 0.25, ALU.mult, ALU.max))
                link(dve.tensor_tensor(g_neg[:, i, :], g_neg[:, i, :], mod[:, m, :], ALU.max))
                link(dve.tensor_tensor(mod[:, m, :], g_neg[:, i, :], g_sign[:, i, :], ALU.mult))
            link(dve.tensor_tensor(ga_bo[:, :], mod[:, 2, :], bo_all[:, :].to_broadcast([P, B]), ALU.mult))
            assert at[0] == SETUP_DVE

            batch(0, True, False, False)
            batch(1, True, True, False)
            with dve.Fori(2, B - 1) as b:
                batch(b, True, True, True)
            batch(B - 1, False, True, True)
            finish(B - 2)
            normalise_heads(B - 1, None)
            residual(B - 1)
            logits_minus_max(B - 1)
            routing(B - 1)
            finish(B - 1)

        @block.scalar
        def _(act):
            def copy_scores(H, par):
                for i, (lo, hi) in enumerate(CHUNKS):
                    act.wait_ge(s["scores"], NC_ * H + i + 1)
                    if i == 0:
                        after(act, s["search"], SEARCH * (H - 2) + 8)
                        after(act, s["e1_done"], 4 * (H - 1))
                    act.activation(S[:, par, lo:hi], pS[:, lo:hi], ACT.Copy).then_inc(s["scopied"], 1)

            def exp_all(H, par):
                act.wait_ge(s["nmax_done"], H + 1)
                after(act, s["pt_full"], NC_ * (H - 1))
                for k, (q, at) in enumerate(TILES):
                    n = P * (q + 1)
                    act.activation(E1[:, par, at:at + n], S[:, par, at:at + n], ACT.Exp,
                                   bias=NMAX[:, par, q:q + 1], scale=SCALE).then_inc(s["e1_done"], 1)

            def exp_rest(H, par):
                for k, (q, at) in enumerate(TILES):
                    n = P * (q + 1)
                    act.wait_ge(s["search"], SEARCH * H + SEARCH - 4 + k + 1)
                    act.activation(E2[:, par, at:at + n], WORK[:, par, at:at + n], ACT.Exp,
                                   bias=NMAX[:, par, q:q + 1], scale=SCALE).then_inc(s["e2_done"], 1)

            def evacuate_probs(H):
                for i, (lo, hi) in enumerate(CHUNKS):
                    act.wait_ge(s["pt_full"], NC_ * H + i + 1)
                    if i == 0:
                        after(act, s["pv_done"], H)
                    act.activation(PT[:, lo:hi], pT[:, 0:hi - lo], ACT.Copy).then_inc(s["pt_evac"], 1)

            def linear_maps(T, t, tp):
                act.wait_ge(s["up1_full"], T + 1)
                act.activation(fa[:, tp, :], F0[:, :], ACT.Identity, bias=W["b1"][:, bass.ds(t, 1)])\
                    .then_inc(s["a_done"], 1)
                act.wait_ge(s["up3_full"], T + 1)
                act.activation(fc[:, tp, :], F1[:, :], ACT.Identity, bias=W["b3"][:, bass.ds(t, 1)])\
                    .then_inc(s["c_done"], 1)
                act.wait_ge(s["u_done"], T + 1)
                act.activation(ft[:, tp, :], fu[:, tp, :], ACT.Tanh, scale=0.5).then_inc(s["t_done"], 1)

            def expert_weights(T, tp):
                act.wait_ge(s["gate_full"], T + 1)
                act.activation(fr[:, tp, :], F0[:, :], ACT.Copy).then_inc(s["r_done"], 1)

            def layer_norm(ln, src, dst, bb, rstd_sem, done):
                act.wait_ge(s[rstd_sem], bb + 1)
                for q in range(NQ):
                    ins = act.activation(dst[:, q, :], src[:, q, :], ACT.Identity, bias=nmr[:, ln, q:q + 1],
                                         scale=rstd[:, ln, q:q + 1])
                ins.then_inc(s[done], 1)

            def modulate_1(bb):
                act.wait_ge(s["ln1T_full"], bb + 1)
                after(act, s["v_full"], bb)
                act.activation(hT[:, :], F1[:, :], ACT.Identity, bias=mod[:, 0, bass.ds(bb, 1)],
                               scale=mod[:, 1, bass.ds(bb, 1)]).then_inc(s["hT_done"], 1)

            def evacuate_kq(bb):
                act.wait_ge(s["kq_full"], 2 * bb + 1)
                after(act, s["scores"], NC_ * NH * bb)
                act.activation(KT[:, :], F0[:, :], ACT.Identity, bias=W["bk"][:, 0:1]).then_inc(s["k_evac"], 1)
                act.wait_ge(s["kq_full"], 2 * bb + 2)
                for j in range(4):
                    ins = act.activation(QT[:, j, :], F1[:, :], ACT.Identity, bias=bq_m[:, j:j + 1],
                                         scale=W["hmask"][:, j:j + 1])
                ins.then_inc(s["q_evac"], 1)

            def evacuate_v(bb):
                act.wait_ge(s["v_full"], bb + 1)
                after(act, s["pv_done"], NH * bb)
                act.activation(VX[:, :, :, 0:DH], F0[:, :].rearrange("p (q h d) -> p q h d", q=NQ, d=DH),
                               ACT.Copy).then_inc(s["v_evac"], 1)

            def attention_out(b):
                act.wait_ge(s["OT_full"], b + 1)
                act.activation(OT[:, :], F0[:, :], ACT.Copy).then_inc(s["OT_evac"], 1)
                act.wait_ge(s["wo_full"], b + 1)
                act.activation(yT[:, :], F1[:, :], ACT.Identity, bias=ga_bo[:, bass.ds(b, 1)],
                               scale=mod[:, 2, bass.ds(b, 1)]).then_inc(s["yT_done"], 1)

            def norm_2(b):
                layer_norm(1, x2, xn2, b, "rstd2", "ln2_done")
                act.wait_ge(s["ln2T_full"], b + 1)
                act.activation(h2T[:, :], F0[:, :], ACT.Identity, bias=mod[:, 3, bass.ds(b, 1)],
                               scale=mod[:, 4, bass.ds(b, 1)]).then_inc(s["h2T_done"], 1)

            def router_exp(b):
                act.wait_ge(s["rsub_done"], b + 1)
                act.activation(rexp[:, :, :], rdif[:, :, :], ACT.Exp).then_inc(s["rexp_done"], 1)

            def route_rows(b):
                act.wait_ge(s["rwT_full"], b + 1)
                act.activation(rwT[:, :], F0[0:E + 1, :], ACT.Copy).then_inc(s["rwT_done"], 1)

            def gate_experts(b):
                act.wait_ge(s["y_full"], b + 1)
                act.activation(zT[:, :], pY[:, :], ACT.Copy, scale=mod[:, 5, bass.ds(b, 1)]).then_inc(s["z_done"], 1)

            def head(b, h, ffn, par):
                H = NH * b + h
                copy_scores(H + 1, 1 - par)
                exp_all(H, par)
                if ffn:
                    T = FT * (b - 1) + h - FIRST_FFN_HEAD
                    tp = (par + FIRST_FFN_HEAD) % 2
                    linear_maps(T, h - FIRST_FFN_HEAD, tp)
                    expert_weights(T, tp)
                evacuate_probs(H - 1)
                exp_rest(H, par)

            def batch(b, prep, ffn):
                H = NH * b
                copy_scores(H + 1, 1)
                exp_all(H, 0)
                if ffn:
                    evacuate_probs(H - 1)
                evacuate_v(b)
                exp_rest(H, 0)
                copy_scores(H + 2, 0)
                exp_all(H + 1, 1)
                if ffn:
                    attention_out(b - 1)
                evacuate_probs(H)
                exp_rest(H + 1, 1)
                copy_scores(H + 3, 1)
                exp_all(H + 2, 0)
                if ffn:
                    norm_2(b - 1)
                if prep:
                    layer_norm(0, xin, xn1, b + 1, "rstd1", "ln1_done")
                evacuate_probs(H + 1)
                exp_rest(H + 2, 0)
                copy_scores(H + 4, 0)
                exp_all(H + 3, 1)
                if ffn:
                    router_exp(b - 1)
                if prep:
                    modulate_1(b + 1)
                if ffn:
                    linear_maps(FT * (b - 1), 0, 0)
                evacuate_probs(H + 2)
                exp_rest(H + 3, 1)
                if ffn:
                    route_rows(b - 1)
                    expert_weights(FT * (b - 1), 0)
                with act.Fori(2, NH // 2 - 1) as p:
                    head(b, 2 * p, ffn, 0)
                    head(b, 2 * p + 1, ffn, 1)
                head(b, NH - 2, ffn, 0)
                if prep:
                    evacuate_kq(b + 1)
                    copy_scores(H + NH, 0)
                exp_all(H + NH - 1, 1)
                if ffn:
                    linear_maps(FT * (b - 1) + FT - 1, FT - 1, 0)
                    expert_weights(FT * (b - 1) + FT - 1, 0)
                evacuate_probs(H + NH - 2)
                exp_rest(H + NH - 1, 1)
                if ffn:
                    gate_experts(b - 1)

            act.wait_ge(s["w_loaded"], n_attn_loads)
            act.activation(c_tanh[:, :], W["cT"][:, :], ACT.Tanh, scale=0.5).then_inc(s["setup_act"], 1)
            layer_norm(0, xin, xn1, 0, "rstd1", "ln1_done")
            act.wait_ge(s["setup_dve"], SETUP_DVE)
            modulate_1(0)
            evacuate_kq(0)
            copy_scores(0, 0)
            act.wait_ge(s["vx_ones"], 1)
            act.wait_ge(s["ffn_loaded"], n_ffn_loads)
            batch(0, True, False)
            with act.Fori(1, B - 1) as b:
                batch(b, True, True)
            batch(B - 1, False, True)
            evacuate_probs(NH * B - 1)
            attention_out(B - 1)
            norm_2(B - 1)
            router_exp(B - 1)
            linear_maps(FT * (B - 1), 0, 0)
            route_rows(B - 1)
            expert_weights(FT * (B - 1), 0)
            with act.Fori(0, (FT - 1) // 2) as i:
                for j in range(2):
                    linear_maps(FT * (B - 1) + 1 + 2 * i + j, 1 + 2 * i + j, 1 - j)
                    expert_weights(FT * (B - 1) + 1 + 2 * i + j, 1 - j)
            gate_experts(B - 1)

        @block.tensor
        def _(pe):
            def four_transposes(dst, src):
                for q in range(NQ):
                    ins = pe.transpose(dst[:, P * q:P * q + P], src[:, q, :] if len(src.shape) == 3
                                       else src[:, P * q:P * q + P], ident[:, :])
                return ins

            def scores(b, h):
                H = NH * b + h
                g, j = h // 4, h % 4
                rows = slice(32 * g, 32 * g + 32)
                for k, (q, at) in enumerate(TILES):
                    n = P * (q + 1)
                    if k != 2:
                        after(pe, s["scopied"], NC_ * (H - 1) + CHUNK_OF[k] + 1)
                    pe.matmul(pS[:, at:at + n], QT[rows, j, P * q:P * q + P], KT[rows, 0:n], start=True, stop=False)
                    ins = pe.matmul(pS[:, at + n - P:at + n], identb[:, :], cmaskb[:, :], start=False, stop=True)
                    if k != 1:
                        ins.then_inc(s["scores"], 1)

            def values(b, h, next_copied):
                H = NH * b + h
                par = h % 2

                def transposes(i):
                    lo, hi = CHUNKS[i]
                    pe.wait_ge(s["p_done"], 4 * H + (1, 3, 4)[i])
                    after(pe, s["pt_evac"], NC_ * H + i)
                    for c in range(lo, hi, P):
                        ins = pe.transpose(pT[:, c - lo:c - lo + P], E1[:, par, c:c + P], ident[:, :])
                    ins.then_inc(s["pt_full"], 1)

                def product(k):
                    q, at = TILES[k]
                    pe.wait_ge(s["pt_evac"], NC_ * H + CHUNK_OF[k] + 1)
                    pe.wait_ge(s["v_evac"], b + 1)
                    for kb in range(q + 1):
                        ins = pe.matmul(o_at[q][:, h * (DH + 1):(h + 1) * (DH + 1)], PT[:, at + P * kb:at + P * kb + P],
                                        VX[:, kb, h, :], start=kb == 0, stop=kb == q)
                    return ins

                transposes(0)
                transposes(1)
                product(0)
                transposes(2)
                product(1)
                pe.wait_ge(s["scopied"], next_copied)
                product(2)
                product(3).then_inc(s["pv_done"], 1)

            def project_kq(bb):
                pe.wait_ge(s["hT_done"], bb + 1)
                pe.matmul(F0[:, :], W["wkT"][:, :], hT[:, :], start=True, stop=True).then_inc(s["kq_full"], 1)
                pe.matmul(F1[:, :], W["wqT"][:, :], hT[:, :], start=True, stop=True).then_inc(s["kq_full"], 1)

            def project_v(bb):
                for q in range(NQ):
                    ins = pe.matmul(F0[:, P * q:P * q + P], hT[:, P * q:P * q + P], W["wvT"][:, :], start=True, stop=True)
                ins.then_inc(s["v_full"], 1)

            def attention_out(b):
                pe.wait_ge(s["norm_done"], b + 1)
                pe.wait_ge(s["v_evac"], min(b + 2, B) if isinstance(b, int) else b + 2)
                four_transposes(F0, osb[:, :, :, :].rearrange("p q h d -> p q (h d)")).then_inc(s["OT_full"], 1)
                pe.wait_ge(s["OT_evac"], b + 1)
                pe.matmul(F1[:, :], W["woT"][:, :], OT[:, :], start=True, stop=True).then_inc(s["wo_full"], 1)
                pe.wait_ge(s["yT_done"], b + 1)
                four_transposes(F0, yT).then_inc(s["att_full"], 1)

            def norm_2_and_logits(b):
                pe.wait_ge(s["ln2_done"], b + 1)
                four_transposes(F0, xn2).then_inc(s["ln2T_full"], 1)
                pe.wait_ge(s["h2T_done"], b + 1)
                for q in range(NQ):
                    ins = pe.matmul(F1[:, E * q:E * q + E], h2T[:, P * q:P * q + P], W["gwT"][:, :], start=True, stop=True)
                ins.then_inc(s["log_full"], 1)

            def norm_1(bb):
                pe.wait_ge(s["ln1_done"], bb + 1)
                four_transposes(F1, xn1).then_inc(s["ln1T_full"], 1)

            def up(T, t):
                pe.matmul(F0[:, :], W["w1"][:, P * t:P * t + P], h2T[:, :], start=True, stop=True)\
                    .then_inc(s["up1_full"], 1)
                if t and t != FT - 1:
                    pe.wait_ge(s["c_done"], T)
                pe.matmul(F1[:, :], W["w3"][:, P * t:P * t + P], h2T[:, :], start=True, stop=True)\
                    .then_inc(s["up3_full"], 1)

            def gate(T, t):
                pe.matmul(F0[:, :], W["sel"][:, P * t:P * t + P], rwT[:, :], start=True, stop=True)\
                    .then_inc(s["gate_full"], 1)

            def down(T, t):
                pe.wait_ge(s["h_done"], T + 1)
                pe.matmul(pY[:, :], W["w2"][:, P * t:P * t + P], fh[:, t % 2, :], start=t == 0, stop=False)\
                    .then_inc(s["w2_done"], 1)

            def expert_tile(b, t, last_copied):
                T = FT * b + t
                if t == 0:
                    pe.wait_ge(s["h2T_done"], b + 1)
                    pe.wait_ge(s["rsub_done"], b + 1)
                else:
                    pe.wait_ge(s["r_done"], T)
                if last_copied is not None:
                    pe.wait_ge(*last_copied)
                elif t == FT - 1:
                    pe.wait_ge(s["c_done"], T)
                up(T, t)
                if t:
                    down(T - 1, t - 1)
                    weights_of(T, t)

            def weights_of(T, t):
                pe.wait_ge(s["a_done"], T + 1)
                gate(T, t)

            def first_weights(b):
                pe.wait_ge(s["rw_done"], b + 1)
                pe.wait_ge(s["a_done"], FT * b + 1)
                four_transposes(F0, rw).then_inc(s["rwT_full"], 1)
                pe.wait_ge(s["rwT_done"], b + 1)
                gate(FT * b, 0)

            def experts_out(b):
                down(FT * b + FT - 1, FT - 1)
                pe.matmul(pY[:, :], W["b2"][:, :], rwT[:, :], start=False, stop=True).then_inc(s["y_full"], 1)
                pe.wait_ge(s["z_done"], b + 1)
                pe.wait_ge(s["c_done"], FT * (b + 1))
                four_transposes(F1, zT).then_inc(s["zT_full"], 1)

            def batch(b, prep, ffn):
                for h in range(NH):
                    H = NH * b + h
                    last = h == NH - 1
                    if last and prep:
                        if ffn:
                            pe.wait_ge(s["r_done"], FT * (b - 1) + FT - 1)
                            pe.wait_ge(s["c_done"], FT * (b - 1) + FT - 1)
                        project_kq(b + 1)
                        pe.wait_ge(s["k_evac"], b + 2)
                        pe.wait_ge(s["q_evac"], b + 2)
                    if ffn and h == 1:
                        pe.wait_ge(s["norm_done"], b)
                    if not last:
                        scores(b, h + 1)
                    elif prep:
                        scores(b + 1, 0)
                    if ffn:
                        if h == 1:
                            attention_out(b - 1)
                        elif h == 2:
                            norm_2_and_logits(b - 1)
                    if h == FIRST_FFN_HEAD and prep:
                        if ffn:
                            pe.wait_ge(s["rsub_done"], b)
                        norm_1(b + 1)
                        pe.wait_ge(s["hT_done"], b + 2)
                    if ffn and h >= FIRST_FFN_HEAD:
                        expert_tile(b - 1, h - FIRST_FFN_HEAD, (s["q_evac"], b + 2) if last and prep else None)
                    copied = NC_ * (H + 2) if prep or not last else NC_ * (H + 1)
                    if h:
                        values(b, h - 1, copied)
                    elif ffn:
                        values(b - 1, NH - 1, copied)
                    if h == 0:
                        project_v(b)
                    if ffn and h == FIRST_FFN_HEAD:
                        first_weights(b - 1)
                if ffn:
                    experts_out(b - 1)

            pe.wait_ge(s["w_loaded"], n_attn_loads)
            pe.wait_ge(s["setup_dve"], 3)
            for m in range(6):
                pe.matmul(F0[:, B * m:B * m + B], W["wmod"][:, D * m:D * m + D], c_silu[:, :], start=True, stop=True)
            pe.matmul(F0[:, 6 * B:6 * B + 1], W["woT"][:, :], W["bv"][:, :], start=True, stop=True)\
                .then_inc(s["setup_pe"], 1)
            norm_1(0)
            pe.wait_ge(s["setup_dve"], SETUP_DVE)
            project_kq(0)
            pe.wait_ge(s["q_evac"], 1)
            pe.wait_ge(s["const_ready"], 3)
            scores(0, 0)
            batch(0, True, False)
            pe.wait_ge(s["ffn_loaded"], n_ffn_loads)
            with pe.Fori(1, B - 1) as b:
                batch(b, True, True)
            batch(B - 1, False, True)
            values(B - 1, NH - 1, NC_ * NH * B)
            attention_out(B - 1)
            norm_2_and_logits(B - 1)
            for t in range(FT):
                expert_tile(B - 1, t, None)
                if t == 0:
                    first_weights(B - 1)
            experts_out(B - 1)


SETUP_DVE = 18
_INS = ["L0_attn_x", "L0_c", "L0_wmod"]


def kernel(**inputs):
    import numpy as np
    import concourse.bacc as bacc
    from concourse.bass_utils import run_bass_kernel_spmd as run

    a = {k: np.asarray(v) for k, v in inputs.items()}

    def col(v):
        return v.reshape(P, 1)

    def hidden(w, sw):
        w = np.concatenate([w, sw[None]], 0).transpose(1, 0, 2).reshape(D, (E + 1) * HID)
        return np.pad(w, ((0, 0), (0, FT * P - w.shape[1])))

    def hidden_col(bv, sbv):
        v = np.concatenate([bv, sbv[None]], 0).reshape(-1)
        return np.pad(v, (0, FT * P - v.size)).reshape(FT, P).T

    w2 = np.concatenate([a["L0_ffn_w2"], a["L0_ffn_sw2"][None]], 0).reshape((E + 1) * HID, D)
    w2 = np.pad(w2, ((0, FT * P - w2.shape[0]), (0, 0))).reshape(FT, P, D).transpose(1, 0, 2).reshape(P, FT * D)
    sel = np.zeros((E + 1, FT * P), np.float32)
    for e in range(E + 1):
        sel[e, e * HID:(e + 1) * HID] = 0.5
    hmask = np.zeros((P, 4), np.float32)
    for r in range(P):
        hmask[r, r // DH % 4] = 1
    w = {
        "cT": a["L0_c"].T, "wmod": a["L0_wmod"], "ident": np.eye(P, dtype=np.float32),
        "cmask": np.triu(np.full((P, P), MASKED, np.float32), 1), "hmask": hmask,
        "wqT": a["L0_attn_Wq"].T, "wkT": a["L0_attn_Wk"].T, "wvT": a["L0_attn_Wv"].T, "woT": a["L0_attn_Wo"].T,
        "bq": col(a["L0_attn_bq"]), "bk": col(a["L0_attn_bk"]), "bv": col(a["L0_attn_bv"]), "bo": col(a["L0_attn_bo"]),
        "gwT": a["L0_ffn_gate_w"].T, "gb": np.tile(a["L0_ffn_gate_b"][None], (P, 1)),
        "iota": np.tile(np.arange(E, dtype=np.float32)[None], (P, 1)),
        "w1": hidden(a["L0_ffn_w1"], a["L0_ffn_sw1"]), "w3": hidden(a["L0_ffn_w3"], a["L0_ffn_sw3"]), "w2": w2,
        "b1": hidden_col(a["L0_ffn_b1"], a["L0_ffn_sb1"]), "b3": hidden_col(a["L0_ffn_b3"], a["L0_ffn_sb3"]),
        "b2": np.concatenate([a["L0_ffn_b2"], a["L0_ffn_sb2"][None]], 0), "sel": sel,
    }
    nc = bacc.Bacc("TRN2", target_bir_lowering=False, num_devices=1)
    arrays = {"in_x": np.ascontiguousarray(a["L0_attn_x"])}
    x_d = nc.dram_tensor("in_x", [B, N, D], F32, kind="ExternalInput").ap()
    w_d = {}
    for name, v in w.items():
        arrays["in_" + name] = np.ascontiguousarray(v)
        w_d[name] = nc.dram_tensor("in_" + name, list(v.shape), F32, kind="ExternalInput").ap()
    out_d = nc.dram_tensor("out", [B, N, D], F32, kind="ExternalOutput").ap()
    build_program(nc, x_d, w_d, out_d)
    r = run(nc, [arrays], core_ids=[0])
    return r.results[0]["out"]
```

```python
from contextlib import ExitStack

import concourse.bass as bass
from concourse import mybir

F32 = mybir.dt.float32
BF16 = mybir.dt.bfloat16
U32 = mybir.dt.uint32
ALU = mybir.AluOpType
ACT = mybir.ActivationFunctionType
AX_X = mybir.AxisListType.X

P = 128
B, N, D = 8, 512, 128
NH, DH, TOP = 16, 8, 32
NQ = N // P
E, HID = 8, 176
FT = -(-(E + 1) * HID // P)
SCALE = DH ** -0.5
EPS = 1e-5
MASKED = -1e30
TAKEN = -1e38

TILES = ((3, 0), (2, 512), (0, 896), (1, 1024))
COLS = sum(P * (q + 1) for q, _ in TILES)
CHUNK_OF = (0, 1, 1, 2)
CHUNKS = ((0, 512), (512, 1024), (1024, 1280))
PAIRS = 8
NC_ = len(CHUNKS)
SEARCH = 2 * 4 * len(TILES)
ROUTE = 12
WHOLE = 32
FIRST_FFN_HEAD = NH - FT


def after(eng, sem, value):
    if isinstance(value, int) and value <= 0:
        return
    eng.wait_ge(sem, value)


def apart(eng, sem, value):
    after(eng, sem, value)
    if not isinstance(value, int):
        eng.nop(nofuse=True)


def build_program(nc, x_d, weights, parts_d, out_d):
    ctx = ExitStack()
    with ctx:
        def sb(name, shape, dt=F32):
            return ctx.enter_context(nc.sbuf_tensor(name, shape, dt))

        def ps(name, shape):
            return ctx.enter_context(nc.psum_tensor(name, shape, F32))

        def sem(name):
            return ctx.enter_context(nc.semaphore(name))

        W = {}
        for name, ap in weights.items():
            W[name] = sb("w_" + name, list(ap.shape))
        ident = W["ident"]
        identb = sb("identb", [P, P], BF16)
        cmaskb = sb("cmaskb", [P, P], BF16)
        c_tanh = sb("c_tanh", [P, B])
        c_half = sb("c_half", [P, B])
        c_silu = sb("c_silu", [P, B])
        mod = sb("mod", [P, 6, B])
        g_sign = sb("g_sign", [P, 2, B])
        g_neg = sb("g_neg", [P, 2, B])
        bo_all = sb("bo_all", [P, 1])
        ga_bo = sb("ga_bo", [P, B])
        minus_half = sb("minus_half", [P, NQ])

        xin = sb("xin", [P, NQ, D])
        xres = sb("xres", [P, NQ, D])
        stats = sb("stats", [P, 2, NQ, 6])
        meanvar = sb("meanvar", [P, 2, NQ, 2])
        veps = sb("veps", [P, 2, NQ])
        rstd = sb("rstd", [P, 2, NQ])
        mrs = sb("mrs", [P, 2, NQ])
        nmr = sb("nmr", [P, 2, NQ])
        xn1 = sb("xn1", [P, NQ, D])
        xn2 = sb("xn2", [P, NQ, D])
        hT = sb("hT", [P, N])
        KQ = sb("KQ", [P, 2, N])
        PART = sb("PART", [P, 2, 3, N], BF16)
        KS = sb("KS", [P, NH // 2, N], BF16)
        QS = sb("QS", [P, NH // 2, N], BF16)
        VX = sb("VX", [P, NQ, NH, DH + 1])
        S = sb("S", [P, 2, COLS])
        WORK = sb("WORK", [P, 2, COLS])
        TOPV = sb("TOPV", [P, 2, NQ, TOP])
        NMAX = sb("NMAX", [P, 2, NQ])
        E1 = sb("E1", [P, 2, COLS])
        E2 = sb("E2", [P, 2, COLS])
        PT = sb("PT", [P, COLS])
        rsum = sb("rsum", [P, NQ, NH])
        osb = sb("osb", [P, NQ, NH, DH])
        OT = sb("OT", [P, N])
        yT = sb("yT", [P, N])
        x2 = sb("x2", [P, NQ, D])

        h2T = sb("h2T", [P, N])
        rmax = sb("rmax", [P, NQ])
        rdif = sb("rdif", [P, NQ, E])
        rexp = sb("rexp", [P, NQ, E])
        rs = sb("rs", [P, NQ])
        rinv = sb("rinv", [P, NQ])
        rscore = sb("rscore", [P, NQ, E])
        rbias = sb("rbias", [P, NQ, E])
        rtop = sb("rtop", [P, NQ, 8])
        ridx = sb("ridx", [P, NQ, 8], U32)
        ridf = sb("ridf", [P, NQ, 2])
        rhit = sb("rhit", [P, 2, NQ, E])
        rw = sb("rw", [P, NQ, P])
        rhb = sb("rhb", [P, 2, NQ, E], BF16)
        rrem = sb("rrem", [P, NQ, E])
        rwT = sb("rwT", [WHOLE + E + 1, N])
        rwTb = sb("rwTb", [3 * (E + 1), N], BF16)
        selb = sb("selb", [3 * (E + 1), FT * P], BF16)
        fa = sb("fa", [P, 2, N])
        fc = sb("fc", [P, 2, N])
        fu = sb("fu", [P, 2, N])
        ft = sb("ft", [P, 2, N])
        ft1 = sb("ft1", [P, 2, N])
        fr = sb("fr", [P, 2, N])
        fv = sb("fv", [P, 2, N])
        fh = sb("fh", [P, 2, N])
        zT = sb("zT", [P, N])
        osum = sb("osum", [P, NQ, D])

        pS = ps("pS", [P, NC_ * 512])
        pT = ps("pT", [P, 512])
        F0 = ps("F0", [P, 512])
        F1 = ps("F1", [P, 512])
        pY = ps("pY", [P, 512])
        pO = ps("pO", [P, 512])
        WO = NH * (DH + 1)
        o_at = {3: pO[:, 0:WO], 2: pO[:, WO:2 * WO], 1: pO[:, 2 * WO:3 * WO], 0: pS[:, COLS:COLS + WO]}

        names = """w_loaded ffn_loaded xin_loaded xres_loaded stored
            const_ready vx_ones rw_ready setup_act setup_dve setup_pe
            scores scopied nmax_done e1_done e2_done search p_done pt_full pt_evac pv_done
            k_full q_full k_evac q_evac k_split q_split split_step parts_stored rsplit sel_ready v_full v_evac
            bn1 rstd1 ln1_done ln1T_full hT_done
            norm_done OT_full OT_evac wo_full yT_done att_full res_done bn2 rstd2 ln2_done ln2T_full h2T_done
            log_full rsub_done rexp_done route rw_done rwT_full rwT_done
            up1_full up3_full gate_full a_done c_done u_done t_done t1_done r_done v_done h_done w2_done
            y_full z_done zT_full fin_done norm_step sub_step pool_step1_in pool_step1 pool_step2"""
        s = {n: sem("s_" + n) for n in names.split()}
        stacked = [sem(f"s_stacked{hp}") for hp in range(NH // 2)]

        ffn_names = ("w1", "w3", "w2", "sel", "b1", "b3", "b2", "gwT", "gb", "iota")
        block = ctx.enter_context(nc.Block())

        def xrows(d, b):
            return d[bass.ds(b, 1), :, :].rearrange("o (q p) d -> p (o q) d", p=P)

        @block.sync
        def _(sp):
            def load_x(b):
                after(sp, s["ln1_done"], b)
                sp.dma_start(xin[:, :, :], xrows(x_d, b)).then_inc(s["xin_loaded"], 16)

            def load_xres(b):
                after(sp, s["res_done"], b)
                sp.dma_start(xres[:, :, :], xrows(x_d, b)).then_inc(s["xres_loaded"], 16)

            def store(b):
                sp.wait_ge(s["fin_done"], b + 1)
                sp.dma_start(xrows(out_d, b), osum[:, :, :]).then_inc(s["stored"], 16)

            def store_parts(bb):
                for hp in range(NH // 2):
                    after(sp, stacked[hp], 64 * bb)
                for side, split in enumerate(("k_split", "q_split")):
                    sp.wait_ge(s[split], bb + 1)
                    for a in range(3):
                        n = min(3, PAIRS - 3 * a)
                        src = PART[:, side, 0:n, :] if side == 0 else \
                            PART[:, side, a:a + 1, :].to_broadcast([P, n, N])
                        sp.dma_start(parts_d[side, 3 * a:3 * a + n, :, :].rearrange("t p n -> p t n"), src)\
                            .then_inc(s["parts_stored"], 16)
                apart(sp, s["parts_stored"], 96 * (bb + 1))

            def load_stacks(bb):
                for hp in range(NH // 2):
                    after(sp, s["scores"], NC_ * (NH * (bb - 1) + 2 * hp + 2))
                    for side, dst in enumerate((KS, QS)):
                        for e in range(2):
                            rows = DH * (2 * hp + e)
                            sp.dma_start(dst[64 * e:64 * e + 64, hp, :], parts_d[side, :, rows:rows + DH, :])\
                                .then_inc(stacked[hp], 16)

            def batch(b, old, next_x, prep):
                if old:
                    store(b - 2)
                load_xres(b)
                if next_x:
                    load_x(b + 2)
                if prep:
                    store_parts(b + 1)
                    load_stacks(b + 1)

            load_x(0)
            for name in weights:
                if name not in ffn_names:
                    sp.dma_start(W[name][:, :], weights[name]).then_inc(s["w_loaded"], 16)
            load_x(1)
            for name in ffn_names[:1]:
                sp.dma_start(W[name][:, :], weights[name]).then_inc(s["ffn_loaded"], 16)
            store_parts(0)
            load_stacks(0)
            for name in ffn_names[1:]:
                sp.dma_start(W[name][:, :], weights[name]).then_inc(s["ffn_loaded"], 16)
            batch(0, False, True, True)
            batch(1, False, True, True)
            with sp.Fori(2, B - 2) as b:
                batch(b, True, True, True)
            batch(B - 2, True, False, True)
            batch(B - 1, True, False, False)
            store(B - 2)
            store(B - 1)
            sp.wait_ge(s["stored"], 16 * B)

        n_attn_loads = 16 * (len(weights) - len(ffn_names))
        n_ffn_loads = 16 * len(ffn_names)

        @block.gpsimd
        def _(pool):
            pool.memset(minus_half[:, :], -0.5).then_inc(s["const_ready"], 1)
            pool.memset(VX[:, :, :, :], 1.0).then_inc(s["vx_ones"], 1)
            pool.memset(rw[:, :, :], 0.0).then_inc(s["rw_ready"], 1)
            pool.wait_ge(s["rw_ready"], 1)
            pool.memset(rw[:, :, E:E + 1], 1.0).then_inc(s["rw_ready"], 1)
            pool.memset(rw[:, :, WHOLE + E:WHOLE + E + 1], 1.0).then_inc(s["rw_ready"], 1)
            pool.wait_ge(s["w_loaded"], n_attn_loads)
            pool.tensor_copy(identb[:, :], ident[:, :]).then_inc(s["const_ready"], 1)
            pool.tensor_copy(cmaskb[:, :], W["cmask"][:, :]).then_inc(s["const_ready"], 1)

            def rsqrt(ln, bb, bn, step, done):
                apart(pool, s[bn], bb + 1)
                pool.tensor_scalar(veps[:, ln, :], meanvar[:, ln, :, 1], EPS, 1.0, ALU.add, ALU.mult).then_inc(s[step], 1)
                pool.wait_ge(s[step], 3 * bb + 1)
                pool.tensor_tensor(rstd[:, ln, :], veps[:, ln, :], minus_half[:, :], ALU.pow).then_inc(s[step], 1)
                pool.wait_ge(s[step], 3 * bb + 2)
                pool.tensor_tensor(mrs[:, ln, :], meanvar[:, ln, :, 0], rstd[:, ln, :], ALU.mult).then_inc(s[step], 1)
                apart(pool, s[step], 3 * bb + 3)
                pool.tensor_scalar(nmr[:, ln, :], mrs[:, ln, :], -1.0, 1.0, ALU.mult, ALU.mult).then_inc(s[done], 1)

            def neg_max(H, par):
                apart(pool, s["search"], SEARCH * H + len(TILES))
                pool.tensor_scalar(NMAX[:, par, :], TOPV[:, par, :, 0], -SCALE, 1.0, ALU.mult,
                                   ALU.mult).then_inc(s["nmax_done"], 1)

            def split(bb, side):
                evac, done = (("k_evac", "k_split"), ("q_evac", "q_split"))[side]
                at = 4 * bb + 2 * side
                pool.wait_ge(s[evac], bb + 1)
                pool.tensor_tensor(KQ[:, side, :], KQ[:, side, :], PART[:, side, 0, :], ALU.subtract)\
                    .then_inc(s["split_step"], 1)
                apart(pool, s["split_step"], at + 1)
                pool.tensor_copy(PART[:, side, 1, :], KQ[:, side, :]).then_inc(s["split_step"], 1)
                pool.wait_ge(s["split_step"], at + 2)
                pool.tensor_tensor(PART[:, side, 2, :], KQ[:, side, :], PART[:, side, 1, :], ALU.subtract)\
                    .then_inc(s[done], 1)

            def split_weights(b):
                whole = rw[:, :, WHOLE:WHOLE + E]
                apart(pool, s["rw_done"], b + 1)
                steps = (lambda: pool.tensor_copy(rhb[:, 0, :, :], whole),
                         lambda: pool.tensor_copy(rw[:, :, 0:E], rhb[:, 0, :, :]),
                         lambda: pool.tensor_tensor(rrem[:, :, :], whole, rhb[:, 0, :, :], ALU.subtract),
                         lambda: pool.tensor_copy(rhb[:, 1, :, :], rrem[:, :, :]),
                         lambda: pool.tensor_copy(rw[:, :, E + 1:2 * E + 1], rhb[:, 1, :, :]),
                         lambda: pool.tensor_tensor(rw[:, :, 2 * E + 2:3 * E + 2], rrem[:, :, :], rhb[:, 1, :, :],
                                                    ALU.subtract))
                for i, step in enumerate(steps):
                    if i:
                        apart(pool, s["rsplit"], len(steps) * b + i)
                    step().then_inc(s["rsplit"], 1)

            def keep_selected(H, par):
                for k, (q, at) in enumerate(TILES):
                    n = P * (q + 1)
                    pool.wait_ge(s["e2_done"], 4 * H + k + 1)
                    pool.tensor_tensor(E1[:, par, at:at + n], E1[:, par, at:at + n], E2[:, par, at:at + n],
                                       ALU.subtract).then_inc(s["p_done"], 1)

            def gate_product(T, tp):
                pool.wait_ge(s["c_done"], T + 1)
                pool.tensor_tensor(fu[:, tp, :], fa[:, tp, :], fc[:, tp, :], ALU.mult).then_inc(s["u_done"], 1)
                apart(pool, s["t_done"], T + 1)
                pool.tensor_scalar(ft1[:, tp, :], ft[:, tp, :], 1.0, 1.0, ALU.add, ALU.mult).then_inc(s["t1_done"], 1)

            def weigh(T, tp):
                pool.wait_ge(s["r_done"], T + 1)
                pool.tensor_tensor(fv[:, tp, :], fu[:, tp, :], fr[:, tp, :], ALU.mult).then_inc(s["v_done"], 1)
                pool.wait_ge(s["v_done"], T + 1)
                pool.tensor_tensor(fh[:, tp, :], fv[:, tp, :], ft1[:, tp, :], ALU.mult).then_inc(s["h_done"], 1)

            def head(b, h, ffn, par):
                H = NH * b + h
                neg_max(H, par)
                if ffn:
                    T = FT * (b - 1) + h - FIRST_FFN_HEAD
                    tp = (par + FIRST_FFN_HEAD) % 2
                    gate_product(T, tp)
                    weigh(T, tp)
                keep_selected(H, par)

            def batch(b, prep, ffn):
                head(b, 0, False, 0)
                head(b, 1, False, 1)
                if ffn:
                    rsqrt(1, b - 1, "bn2", "pool_step2", "rstd2")
                if prep:
                    rsqrt(0, b + 1, "bn1", "pool_step1", "rstd1")
                head(b, 2, False, 0)
                neg_max(NH * b + 3, 1)
                if prep:
                    split(b + 1, 0)
                    split(b + 1, 1)
                if ffn:
                    gate_product(FT * (b - 1), 0)
                keep_selected(NH * b + 3, 1)
                if ffn:
                    split_weights(b - 1)
                    weigh(FT * (b - 1), 0)
                with pool.Fori(2, NH // 2) as p:
                    head(b, 2 * p, ffn, 0)
                    head(b, 2 * p + 1, ffn, 1)

            rsqrt(0, 0, "bn1", "pool_step1", "rstd1")
            split(0, 0)
            split(0, 1)
            pool.wait_ge(s["ffn_loaded"], n_ffn_loads)
            pool.tensor_copy(selb[:, :], W["sel"][:, :]).then_inc(s["sel_ready"], 1)
            batch(0, True, False)
            with pool.Fori(1, B - 1) as b:
                batch(b, True, True)
            batch(B - 1, False, True)
            rsqrt(1, B - 1, "bn2", "pool_step2", "rstd2")
            gate_product(FT * (B - 1), 0)
            split_weights(B - 1)
            weigh(FT * (B - 1), 0)
            with pool.Fori(0, (FT - 1) // 2) as i:
                for j in range(2):
                    T = FT * (B - 1) + 1 + 2 * i + j
                    gate_product(T, 1 - j)
                    weigh(T, 1 - j)

        @block.vector
        def _(dve):
            def head(b, h, par):
                H = NH * b + h
                for r in range(TOP // 8):
                    for k, (q, at) in enumerate(TILES):
                        n = P * (q + 1)
                        src = (WORK if r else S)[:, par, at:at + n]
                        if r == 0:
                            if k == 0:
                                apart(dve, s["nmax_done"], H - 1)
                            apart(dve, s["scopied"], NC_ * H + CHUNK_OF[k] + 1)
                        else:
                            apart(dve, s["search"], SEARCH * H + 8 * r - 4 + k + 1)
                        dve.max(TOPV[:, par, q, 8 * r:8 * r + 8], src).then_inc(s["search"], 1)
                    for k, (q, at) in enumerate(TILES):
                        n = P * (q + 1)
                        src = (WORK if r else S)[:, par, at:at + n]
                        if r == 0:
                            apart(dve, s["e2_done"], 4 * (H - 2) + k + 1)
                        apart(dve, s["search"], SEARCH * H + 8 * r + k + 1)
                        dve.match_replace(out=WORK[:, par, at:at + n], in_to_replace=TOPV[:, par, q, 8 * r:8 * r + 8],
                                          in_values=src, imm_value=TAKEN).then_inc(s["search"], 1)

            def statistics(ln, src, bb, step, done):
                for q in range(NQ):
                    dve.bn_stats(stats[:, ln, q, :], src[:, q, :]).then_inc(s[step], 1)
                for q in range(NQ):
                    apart(dve, s[step], 4 * bb + q + 1)
                    last = dve.bn_aggr(meanvar[:, ln, q, :], stats[:, ln, q, :])
                last.then_inc(s[done], 1)

            def normalise_heads(b, prev_scores):
                dve.wait_ge(s["pv_done"], NH * (b + 1))
                if prev_scores is not None:
                    dve.wait_ge(s["scopied"], prev_scores)
                big = pO[:, 0:3 * WO].rearrange("p (q h c) -> p q h c", q=3, c=DH + 1)
                small = pS[:, COLS:COLS + WO].rearrange("p (h c) -> p h c", c=DH + 1)
                dve.reciprocal(rsum[:, 1:4, :], big[:, :, :, DH]).then_inc(s["norm_step"], 1)
                dve.reciprocal(rsum[:, 0, :], small[:, :, DH]).then_inc(s["norm_step"], 1)
                after(dve, s["OT_full"], b)
                dve.wait_ge(s["norm_step"], 2 * b + 1)
                for i, q in enumerate((3, 2, 1)):
                    dve.tensor_tensor(osb[:, q, :, :], big[:, i, :, 0:DH],
                                      rsum[:, 1 + i, :].unsqueeze(2).to_broadcast([P, NH, DH]), ALU.mult)
                dve.wait_ge(s["norm_step"], 2 * b + 2)
                dve.tensor_tensor(osb[:, 0, :, :], small[:, :, 0:DH],
                                  rsum[:, 0, :].unsqueeze(2).to_broadcast([P, NH, DH]),
                                  ALU.mult).then_inc(s["norm_done"], 1)

            def finish(fb):
                dve.wait_ge(s["zT_full"], fb + 1)
                after(dve, s["stored"], 16 * fb)
                dve.tensor_tensor(osum[:, :, :], x2[:, :, :], F1[:, :].rearrange("p (q d) -> p q d", q=NQ),
                                  ALU.add).then_inc(s["fin_done"], 1)

            def residual(b):
                dve.wait_ge(s["att_full"], b + 1)
                dve.wait_ge(s["xres_loaded"], 16 * (b + 1))
                dve.tensor_tensor(x2[:, :, :], xres[:, :, :], F0[:, :].rearrange("p (q d) -> p q d", q=NQ),
                                  ALU.add).then_inc(s["res_done"], 1)
                apart(dve, s["res_done"], b + 1)
                statistics(1, x2, b, "sub_step", "bn2")

            def logits_minus_max(b):
                logits = F1[:, 0:NQ * E].rearrange("p (q e) -> p q e", q=NQ)
                dve.wait_ge(s["log_full"], b + 1)
                dve.tensor_reduce(rmax[:, :], logits, AX_X, ALU.max).then_inc(s["route"], 1)
                dve.wait_ge(s["route"], ROUTE * b + 1)
                dve.tensor_tensor(rdif[:, :, :], logits, rmax[:, :].unsqueeze(2).to_broadcast([P, NQ, E]),
                                  ALU.subtract).then_inc(s["rsub_done"], 1)

            def routing(b):
                at = [ROUTE * b + 1]

                def step(ins):
                    ins.then_inc(s["route"], 1)
                    at[0] = at[0] + 1

                def settle():
                    apart(dve, s["route"], at[0])

                dve.wait_ge(s["rexp_done"], b + 1)
                dve.wait_ge(s["ffn_loaded"], n_ffn_loads)
                step(dve.tensor_reduce(rs[:, :], rexp[:, :, :], AX_X, ALU.add))
                settle()
                step(dve.reciprocal(rinv[:, :], rs[:, :]))
                settle()
                step(dve.tensor_tensor(rscore[:, :, :], rexp[:, :, :],
                                       rinv[:, :].unsqueeze(2).to_broadcast([P, NQ, E]), ALU.mult))
                settle()
                step(dve.tensor_tensor(rbias[:, :, :], rscore[:, :, :],
                                       W["gb"][:, :].unsqueeze(1).to_broadcast([P, NQ, E]), ALU.add))
                settle()
                for q in range(NQ):
                    ins = dve.max(rtop[:, q, :], rbias[:, q, :])
                step(ins)
                settle()
                for q in range(NQ):
                    ins = dve.max_index(ridx[:, q, :], rtop[:, q, :], rbias[:, q, :])
                step(ins)
                settle()
                step(dve.tensor_copy(ridf[:, :, :], ridx[:, :, 0:2]))
                settle()
                for i in range(2):
                    step(dve.tensor_tensor(rhit[:, i, :, :], ridf[:, :, i:i + 1].to_broadcast([P, NQ, E]),
                                           W["iota"][:, :].unsqueeze(1).to_broadcast([P, NQ, E]), ALU.is_equal))
                settle()
                step(dve.tensor_tensor(rhit[:, 0, :, :], rhit[:, 0, :, :], rhit[:, 1, :, :], ALU.add))
                settle()
                step(dve.tensor_tensor(rdif[:, :, :], rhit[:, 0, :, :], rscore[:, :, :], ALU.mult))
                settle()
                after(dve, s["rwT_full"], b)
                if not isinstance(b, int) or b == 0:
                    dve.wait_ge(s["rw_ready"], 3)
                dve.tensor_copy(rw[:, :, WHOLE:WHOLE + E], rdif[:, :, :]).then_inc(s["rw_done"], 1)

            def batch(b, prep, ffn, old):
                head(b, 0, 0)
                if old:
                    finish(b - 2)
                if ffn:
                    normalise_heads(b - 1, NC_ * (NH * b + 1) + NC_)
                head(b, 1, 1)
                if ffn:
                    residual(b - 1)
                if prep:
                    dve.wait_ge(s["xin_loaded"], 16 * (b + 2))
                    statistics(0, xin, b + 1, "pool_step1_in", "bn1")
                head(b, 2, 0)
                if ffn:
                    logits_minus_max(b - 1)
                head(b, 3, 1)
                if ffn:
                    routing(b - 1)
                with dve.Fori(2, NH // 2) as p:
                    head(b, 2 * p, 0)
                    head(b, 2 * p + 1, 1)

            at = [0]

            def link(ins):
                at[0] += 1
                ins.then_inc(s["setup_dve"], 1)
                dve.wait_ge(s["setup_dve"], at[0])

            dve.wait_ge(s["xin_loaded"], 16)
            statistics(0, xin, 0, "pool_step1_in", "bn1")
            dve.wait_ge(s["setup_act"], 1)
            link(dve.tensor_scalar(c_half[:, :], W["cT"][:, :], 0.5, None, ALU.mult))
            link(dve.scalar_tensor_tensor(out=c_silu[:, :], in0=c_tanh[:, :], scalar=1.0, in1=c_half[:, :],
                                          op0=ALU.add, op1=ALU.mult))
            dve.wait_ge(s["setup_pe"], 1)
            link(dve.tensor_copy(mod[:, :, :], F0[:, 0:6 * B].rearrange("p (m b) -> p m b", m=6)))
            link(dve.tensor_tensor(bo_all[:, :], W["bo"][:, :], F0[:, 6 * B:6 * B + 1], ALU.add))
            for i in (1, 4):
                link(dve.tensor_scalar(mod[:, i, :], mod[:, i, :], 1.0, None, ALU.add))
            for i, m in enumerate((2, 5)):
                link(dve.tensor_scalar(g_sign[:, i, :], mod[:, m, :], 0.0, 2.0, ALU.is_ge, ALU.mult))
                link(dve.tensor_scalar(g_sign[:, i, :], g_sign[:, i, :], -1.0, None, ALU.add))
                link(dve.tensor_scalar(g_neg[:, i, :], mod[:, m, :], -1.0, 0.25, ALU.mult, ALU.max))
                link(dve.tensor_tensor(g_neg[:, i, :], g_neg[:, i, :], mod[:, m, :], ALU.max))
                link(dve.tensor_tensor(mod[:, m, :], g_neg[:, i, :], g_sign[:, i, :], ALU.mult))
            link(dve.tensor_tensor(ga_bo[:, :], mod[:, 2, :], bo_all[:, :].to_broadcast([P, B]), ALU.mult))
            assert at[0] == SETUP_DVE

            batch(0, True, False, False)
            batch(1, True, True, False)
            with dve.Fori(2, B - 1) as b:
                batch(b, True, True, True)
            batch(B - 1, False, True, True)
            finish(B - 2)
            normalise_heads(B - 1, None)
            residual(B - 1)
            logits_minus_max(B - 1)
            routing(B - 1)
            finish(B - 1)

        @block.scalar
        def _(act):
            def copy_scores(H, par):
                for i, (lo, hi) in enumerate(CHUNKS):
                    act.wait_ge(s["scores"], NC_ * H + i + 1)
                    if i == 0:
                        after(act, s["search"], SEARCH * (H - 2) + 8)
                        after(act, s["e1_done"], 4 * (H - 1))
                    act.activation(S[:, par, lo:hi], pS[:, lo:hi], ACT.Copy).then_inc(s["scopied"], 1)

            def exp_all(H, par):
                act.wait_ge(s["nmax_done"], H + 1)
                after(act, s["pt_full"], NC_ * (H - 1))
                for k, (q, at) in enumerate(TILES):
                    n = P * (q + 1)
                    act.activation(E1[:, par, at:at + n], S[:, par, at:at + n], ACT.Exp,
                                   bias=NMAX[:, par, q:q + 1], scale=SCALE).then_inc(s["e1_done"], 1)

            def exp_rest(H, par):
                for k, (q, at) in enumerate(TILES):
                    n = P * (q + 1)
                    act.wait_ge(s["search"], SEARCH * H + SEARCH - 4 + k + 1)
                    act.activation(E2[:, par, at:at + n], WORK[:, par, at:at + n], ACT.Exp,
                                   bias=NMAX[:, par, q:q + 1], scale=SCALE).then_inc(s["e2_done"], 1)

            def evacuate_chunk(H, i):
                lo, hi = CHUNKS[i]
                act.wait_ge(s["pt_full"], NC_ * H + i + 1)
                if i == 0:
                    after(act, s["pv_done"], H)
                act.activation(PT[:, lo:hi], pT[:, 0:hi - lo], ACT.Copy).then_inc(s["pt_evac"], 1)

            def evacuate_probs(H):
                for i in range(NC_):
                    evacuate_chunk(H, i)

            def linear_1(T, t, tp):
                act.wait_ge(s["up1_full"], T + 1)
                act.activation(fa[:, tp, :], F0[:, :], ACT.Identity, bias=W["b1"][:, bass.ds(t, 1)])\
                    .then_inc(s["a_done"], 1)

            def linear_3(T, t, tp):
                act.wait_ge(s["up3_full"], T + 1)
                act.activation(fc[:, tp, :], F1[:, :], ACT.Identity, bias=W["b3"][:, bass.ds(t, 1)])\
                    .then_inc(s["c_done"], 1)

            def half_tanh(T, tp):
                act.wait_ge(s["u_done"], T + 1)
                act.activation(ft[:, tp, :], fu[:, tp, :], ACT.Tanh, scale=0.5).then_inc(s["t_done"], 1)

            def linear_maps(T, t, tp):
                linear_1(T, t, tp)
                linear_3(T, t, tp)
                half_tanh(T, tp)

            def expert_weights(T, tp):
                act.wait_ge(s["gate_full"], T + 1)
                act.activation(fr[:, tp, :], F0[:, :], ACT.Copy).then_inc(s["r_done"], 1)

            def layer_norm(ln, src, dst, bb, rstd_sem, done):
                act.wait_ge(s[rstd_sem], bb + 1)
                for q in range(NQ):
                    ins = act.activation(dst[:, q, :], src[:, q, :], ACT.Identity, bias=nmr[:, ln, q:q + 1],
                                         scale=rstd[:, ln, q:q + 1])
                ins.then_inc(s[done], 1)

            def modulate_1(bb):
                act.wait_ge(s["ln1T_full"], bb + 1)
                after(act, s["v_full"], bb)
                act.activation(hT[:, :], F1[:, :], ACT.Identity, bias=mod[:, 0, bass.ds(bb, 1)],
                               scale=mod[:, 1, bass.ds(bb, 1)]).then_inc(s["hT_done"], 1)

            def evacuate_kq(bb):
                for side, (full, bank, bias, done) in enumerate(
                        (("k_full", F0, "bk", "k_evac"), ("q_full", F1, "bq", "q_evac"))):
                    act.wait_ge(s[full], bb + 1)
                    after(act, s["parts_stored"], 96 * bb)
                    act.activation(KQ[:, side, :], bank[:, :], ACT.Identity, bias=W[bias][:, 0:1])
                    act.activation(PART[:, side, 0, :], bank[:, :], ACT.Identity, bias=W[bias][:, 0:1])\
                        .then_inc(s[done], 1)

            def evacuate_v(bb):
                act.wait_ge(s["v_full"], bb + 1)
                after(act, s["pv_done"], NH * bb)
                act.activation(VX[:, :, :, 0:DH], F0[:, :].rearrange("p (q h d) -> p q h d", q=NQ, d=DH),
                               ACT.Copy).then_inc(s["v_evac"], 1)

            def attention_out(b):
                act.wait_ge(s["OT_full"], b + 1)
                act.activation(OT[:, :], F0[:, :], ACT.Copy).then_inc(s["OT_evac"], 1)
                act.wait_ge(s["wo_full"], b + 1)
                act.activation(yT[:, :], F1[:, :], ACT.Identity, bias=ga_bo[:, bass.ds(b, 1)],
                               scale=mod[:, 2, bass.ds(b, 1)]).then_inc(s["yT_done"], 1)

            def norm_2(b):
                layer_norm(1, x2, xn2, b, "rstd2", "ln2_done")
                act.wait_ge(s["ln2T_full"], b + 1)
                act.activation(h2T[:, :], F0[:, :], ACT.Identity, bias=mod[:, 3, bass.ds(b, 1)],
                               scale=mod[:, 4, bass.ds(b, 1)]).then_inc(s["h2T_done"], 1)

            def router_exp(b):
                act.wait_ge(s["rsub_done"], b + 1)
                act.activation(rexp[:, :, :], rdif[:, :, :], ACT.Exp).then_inc(s["rexp_done"], 1)

            def route_rows(b):
                act.wait_ge(s["rwT_full"], b + 1)
                act.activation(rwTb[:, :], F0[0:3 * (E + 1), :], ACT.Copy)
                act.activation(rwT[WHOLE:WHOLE + E + 1, :], F0[WHOLE:WHOLE + E + 1, :], ACT.Copy)\
                    .then_inc(s["rwT_done"], 1)

            def gate_experts(b):
                act.wait_ge(s["y_full"], b + 1)
                act.activation(zT[:, :], pY[:, :], ACT.Copy, scale=mod[:, 5, bass.ds(b, 1)]).then_inc(s["z_done"], 1)

            def head(b, h, ffn, par, more=True):
                H = NH * b + h
                if more:
                    copy_scores(H + 1, 1 - par)
                if ffn:
                    T = FT * (b - 1) + h - FIRST_FFN_HEAD
                    tp = (par + FIRST_FFN_HEAD) % 2
                    linear_1(T, h - FIRST_FFN_HEAD, tp)
                    evacuate_chunk(H - 1, 0)
                    linear_3(T, h - FIRST_FFN_HEAD, tp)
                    exp_all(H, par)
                    evacuate_chunk(H - 1, 1)
                    half_tanh(T, tp)
                    evacuate_chunk(H - 1, 2)
                    expert_weights(T, tp)
                else:
                    exp_all(H, par)
                    evacuate_probs(H - 1)
                exp_rest(H, par)

            def batch(b, prep, ffn, old):
                H = NH * b
                copy_scores(H + 1, 1)
                exp_all(H, 0)
                if ffn:
                    evacuate_probs(H - 1)
                evacuate_v(b)
                if old:
                    gate_experts(b - 2)
                exp_rest(H, 0)
                copy_scores(H + 2, 0)
                exp_all(H + 1, 1)
                if ffn:
                    attention_out(b - 1)
                evacuate_probs(H)
                exp_rest(H + 1, 1)
                copy_scores(H + 3, 1)
                exp_all(H + 2, 0)
                if ffn:
                    norm_2(b - 1)
                if prep:
                    layer_norm(0, xin, xn1, b + 1, "rstd1", "ln1_done")
                evacuate_probs(H + 1)
                exp_rest(H + 2, 0)
                copy_scores(H + 4, 0)
                exp_all(H + 3, 1)
                if ffn:
                    router_exp(b - 1)
                if prep:
                    modulate_1(b + 1)
                    evacuate_kq(b + 1)
                if ffn:
                    linear_maps(FT * (b - 1), 0, 0)
                evacuate_probs(H + 2)
                exp_rest(H + 3, 1)
                if ffn:
                    route_rows(b - 1)
                    expert_weights(FT * (b - 1), 0)
                with act.Fori(2, NH // 2 - 1) as p:
                    head(b, 2 * p, ffn, 0)
                    head(b, 2 * p + 1, ffn, 1)
                head(b, NH - 2, ffn, 0)
                head(b, NH - 1, ffn, 1, more=prep)

            act.wait_ge(s["w_loaded"], n_attn_loads)
            act.activation(c_tanh[:, :], W["cT"][:, :], ACT.Tanh, scale=0.5).then_inc(s["setup_act"], 1)
            layer_norm(0, xin, xn1, 0, "rstd1", "ln1_done")
            act.wait_ge(s["setup_dve"], SETUP_DVE)
            modulate_1(0)
            evacuate_kq(0)
            copy_scores(0, 0)
            act.wait_ge(s["vx_ones"], 1)
            act.wait_ge(s["ffn_loaded"], n_ffn_loads)
            batch(0, True, False, False)
            batch(1, True, True, False)
            with act.Fori(2, B - 1) as b:
                batch(b, True, True, True)
            batch(B - 1, False, True, True)
            evacuate_probs(NH * B - 1)
            gate_experts(B - 2)
            attention_out(B - 1)
            norm_2(B - 1)
            router_exp(B - 1)
            linear_maps(FT * (B - 1), 0, 0)
            route_rows(B - 1)
            expert_weights(FT * (B - 1), 0)
            with act.Fori(0, (FT - 1) // 2) as i:
                for j in range(2):
                    linear_maps(FT * (B - 1) + 1 + 2 * i + j, 1 + 2 * i + j, 1 - j)
                    expert_weights(FT * (B - 1) + 1 + 2 * i + j, 1 - j)
            gate_experts(B - 1)

        @block.tensor
        def _(pe):
            def four_transposes(dst, src):
                for q in range(NQ):
                    ins = pe.transpose(dst[:, P * q:P * q + P], src[:, q, :] if len(src.shape) == 3
                                       else src[:, P * q:P * q + P], ident[:, :])
                return ins

            def scores(b, h):
                H = NH * b + h
                rows = slice(64 * (h % 2), 64 * (h % 2) + 64)
                if h % 2 == 0:
                    pe.wait_ge(stacked[h // 2], 64 * (b + 1))
                for k, (q, at) in enumerate(TILES):
                    n = P * (q + 1)
                    if k != 2:
                        after(pe, s["scopied"], NC_ * (H - 1) + CHUNK_OF[k] + 1)
                    pe.matmul(pS[:, at:at + n], QS[rows, h // 2, P * q:P * q + P], KS[rows, h // 2, 0:n], start=True, stop=False)
                    ins = pe.matmul(pS[:, at + n - P:at + n], identb[:, :], cmaskb[:, :], start=False, stop=True)
                    if k != 1:
                        ins.then_inc(s["scores"], 1)

            def values(b, h, next_copied):
                H = NH * b + h
                par = h % 2

                def transposes(i):
                    lo, hi = CHUNKS[i]
                    pe.wait_ge(s["p_done"], 4 * H + (1, 3, 4)[i])
                    after(pe, s["pt_evac"], NC_ * H + i)
                    for c in range(lo, hi, P):
                        ins = pe.transpose(pT[:, c - lo:c - lo + P], E1[:, par, c:c + P], ident[:, :])
                    ins.then_inc(s["pt_full"], 1)

                def product(k):
                    q, at = TILES[k]
                    pe.wait_ge(s["pt_evac"], NC_ * H + CHUNK_OF[k] + 1)
                    pe.wait_ge(s["v_evac"], b + 1)
                    for kb in range(q + 1):
                        ins = pe.matmul(o_at[q][:, h * (DH + 1):(h + 1) * (DH + 1)], PT[:, at + P * kb:at + P * kb + P],
                                        VX[:, kb, h, :], start=kb == 0, stop=kb == q)
                    return ins

                transposes(0)
                yield
                transposes(1)
                product(0)
                yield
                transposes(2)
                product(1)
                yield
                pe.wait_ge(s["scopied"], next_copied)
                product(2)
                product(3).then_inc(s["pv_done"], 1)
                yield

            def project_kq(bb):
                pe.wait_ge(s["hT_done"], bb + 1)
                pe.matmul(F0[:, :], W["wkT"][:, :], hT[:, :], start=True, stop=True).then_inc(s["k_full"], 1)
                pe.matmul(F1[:, :], W["wqT"][:, :], hT[:, :], start=True, stop=True).then_inc(s["q_full"], 1)

            def project_v(bb):
                for q in range(NQ):
                    ins = pe.matmul(F0[:, P * q:P * q + P], hT[:, P * q:P * q + P], W["wvT"][:, :], start=True, stop=True)
                ins.then_inc(s["v_full"], 1)

            def attention_out(b):
                pe.wait_ge(s["norm_done"], b + 1)
                if not (isinstance(b, int) and b == B - 1):
                    pe.wait_ge(s["v_evac"], b + 2)
                four_transposes(F0, osb[:, :, :, :].rearrange("p q h d -> p q (h d)")).then_inc(s["OT_full"], 1)
                pe.wait_ge(s["OT_evac"], b + 1)
                pe.matmul(F1[:, :], W["woT"][:, :], OT[:, :], start=True, stop=True).then_inc(s["wo_full"], 1)
                pe.wait_ge(s["yT_done"], b + 1)
                four_transposes(F0, yT).then_inc(s["att_full"], 1)

            def norm_2_and_logits(b):
                pe.wait_ge(s["ln2_done"], b + 1)
                four_transposes(F0, xn2).then_inc(s["ln2T_full"], 1)
                pe.wait_ge(s["h2T_done"], b + 1)
                for q in range(NQ):
                    ins = pe.matmul(F1[:, E * q:E * q + E], h2T[:, P * q:P * q + P], W["gwT"][:, :], start=True, stop=True)
                ins.then_inc(s["log_full"], 1)

            def norm_1(bb):
                pe.wait_ge(s["ln1_done"], bb + 1)
                four_transposes(F1, xn1).then_inc(s["ln1T_full"], 1)

            def up1(T, t):
                pe.matmul(F0[:, :], W["w1"][:, P * t:P * t + P], h2T[:, :], start=True, stop=True)\
                    .then_inc(s["up1_full"], 1)

            def up3(T, t):
                pe.matmul(F1[:, :], W["w3"][:, P * t:P * t + P], h2T[:, :], start=True, stop=True)\
                    .then_inc(s["up3_full"], 1)

            def gate(T, t):
                pe.matmul(F0[:, :], selb[:, P * t:P * t + P], rwTb[:, :], start=True, stop=True)\
                    .then_inc(s["gate_full"], 1)

            def down(T, t):
                pe.wait_ge(s["h_done"], T + 1)
                pe.matmul(pY[:, :], W["w2"][:, P * t:P * t + P], fh[:, t % 2, :], start=t == 0, stop=False)\
                    .then_inc(s["w2_done"], 1)

            def first_tile(b, prep):
                pe.wait_ge(s["h2T_done"], b + 1)
                if prep:
                    pe.wait_ge(s["k_evac"], b + 3)
                    pe.wait_ge(s["q_evac"], b + 3)
                else:
                    pe.wait_ge(s["rsub_done"], b + 1)
                up1(FT * b, 0)
                up3(FT * b, 0)

            def expert_tile(b, t):
                T = FT * b + t
                pe.wait_ge(s["r_done"], T)
                up1(T, t)
                yield
                pe.wait_ge(s["c_done"], T)
                up3(T, t)
                yield
                down(T - 1, t - 1)
                yield
                weights_of(T, t)
                yield

            def weights_of(T, t):
                pe.wait_ge(s["a_done"], T + 1)
                gate(T, t)

            def first_weights(b):
                pe.wait_ge(s["rsplit"], 6 * (b + 1))
                pe.wait_ge(s["a_done"], FT * b + 1)
                four_transposes(F0, rw).then_inc(s["rwT_full"], 1)
                pe.wait_ge(s["rwT_done"], b + 1)
                gate(FT * b, 0)

            def experts_out(b):
                down(FT * b + FT - 1, FT - 1)
                pe.matmul(pY[:, :], W["b2"][WHOLE:WHOLE + E + 1, :], rwT[WHOLE:WHOLE + E + 1, :], start=False, stop=True).then_inc(s["y_full"], 1)
                pe.wait_ge(s["z_done"], b + 1)
                pe.wait_ge(s["c_done"], FT * (b + 1))
                four_transposes(F1, zT).then_inc(s["zT_full"], 1)

            def run(*pieces):
                for _ in zip(*pieces, strict=True):
                    pass

            def batch(b, prep, ffn, old):
                for h in range(NH):
                    H = NH * b + h
                    last = h == NH - 1
                    if ffn and h == 1:
                        pe.wait_ge(s["norm_done"], b)
                    if not last:
                        scores(b, h + 1)
                    elif prep:
                        scores(b + 1, 0)
                    if ffn:
                        if h == 1:
                            attention_out(b - 1)
                        elif h == 2:
                            norm_2_and_logits(b - 1)
                    if h == FIRST_FFN_HEAD:
                        if prep:
                            if ffn:
                                pe.wait_ge(s["rsub_done"], b)
                            norm_1(b + 1)
                            project_kq(b + 1)
                        if ffn:
                            first_tile(b - 1, prep)
                    copied = NC_ * (H + 2) if prep or not last else NC_ * (H + 1)
                    if h > FIRST_FFN_HEAD and ffn:
                        run(expert_tile(b - 1, h - FIRST_FFN_HEAD), values(b, h - 1, copied))
                    elif h:
                        run(values(b, h - 1, copied))
                    elif ffn:
                        run(values(b - 1, NH - 1, copied))
                    if h == 0:
                        pe.wait_ge(s["k_evac"], b + 1)
                        if old:
                            pe.wait_ge(s["r_done"], FT * (b - 1))
                        project_v(b)
                        if old:
                            experts_out(b - 2)
                    if ffn and h == FIRST_FFN_HEAD:
                        first_weights(b - 1)

            pe.wait_ge(s["w_loaded"], n_attn_loads)
            pe.wait_ge(s["setup_dve"], 2)
            for m in range(6):
                pe.matmul(F0[:, B * m:B * m + B], W["wmod"][:, D * m:D * m + D], c_silu[:, :], start=True, stop=True)
            pe.matmul(F0[:, 6 * B:6 * B + 1], W["woT"][:, :], W["bv"][:, :], start=True, stop=True)\
                .then_inc(s["setup_pe"], 1)
            norm_1(0)
            pe.wait_ge(s["setup_dve"], SETUP_DVE)
            project_kq(0)
            pe.wait_ge(s["const_ready"], 3)
            scores(0, 0)
            batch(0, True, False, False)
            pe.wait_ge(s["ffn_loaded"], n_ffn_loads)
            pe.wait_ge(s["sel_ready"], 1)
            batch(1, True, True, False)
            with pe.Fori(2, B - 1) as b:
                batch(b, True, True, True)
            batch(B - 1, False, True, True)
            run(values(B - 1, NH - 1, NC_ * NH * B))
            experts_out(B - 2)
            attention_out(B - 1)
            norm_2_and_logits(B - 1)
            first_tile(B - 1, False)
            first_weights(B - 1)
            for t in range(1, FT):
                run(expert_tile(B - 1, t))
            experts_out(B - 1)


SETUP_DVE = 17
_INS = ["L0_attn_x", "L0_c", "L0_wmod"]


def kernel(**inputs):
    import numpy as np
    import concourse.bacc as bacc
    from concourse.bass_utils import run_bass_kernel_spmd as run

    a = {k: np.asarray(v) for k, v in inputs.items()}

    def col(v):
        return v.reshape(P, 1)

    def hidden(w, sw):
        w = np.concatenate([w, sw[None]], 0).transpose(1, 0, 2).reshape(D, (E + 1) * HID)
        return np.pad(w, ((0, 0), (0, FT * P - w.shape[1])))

    def hidden_col(bv, sbv):
        v = np.concatenate([bv, sbv[None]], 0).reshape(-1)
        return np.pad(v, (0, FT * P - v.size)).reshape(FT, P).T

    w2 = np.concatenate([a["L0_ffn_w2"], a["L0_ffn_sw2"][None]], 0).reshape((E + 1) * HID, D)
    w2 = np.pad(w2, ((0, FT * P - w2.shape[0]), (0, 0))).reshape(FT, P, D).transpose(1, 0, 2).reshape(P, FT * D)
    sel = np.zeros((E + 1, FT * P), np.float32)
    for e in range(E + 1):
        sel[e, e * HID:(e + 1) * HID] = 0.5
    b2 = np.concatenate([a["L0_ffn_b2"], a["L0_ffn_sb2"][None]], 0)
    w = {
        "cT": a["L0_c"].T, "wmod": a["L0_wmod"], "ident": np.eye(P, dtype=np.float32),
        "cmask": np.triu(np.full((P, P), MASKED, np.float32), 1),
        "wqT": a["L0_attn_Wq"].T, "wkT": a["L0_attn_Wk"].T, "wvT": a["L0_attn_Wv"].T, "woT": a["L0_attn_Wo"].T,
        "bq": col(a["L0_attn_bq"]), "bk": col(a["L0_attn_bk"]), "bv": col(a["L0_attn_bv"]), "bo": col(a["L0_attn_bo"]),
        "gwT": a["L0_ffn_gate_w"].T, "gb": np.tile(a["L0_ffn_gate_b"][None], (P, 1)),
        "iota": np.tile(np.arange(E, dtype=np.float32)[None], (P, 1)),
        "w1": hidden(a["L0_ffn_w1"], a["L0_ffn_sw1"]), "w3": hidden(a["L0_ffn_w3"], a["L0_ffn_sw3"]), "w2": w2,
        "b1": hidden_col(a["L0_ffn_b1"], a["L0_ffn_sb1"]), "b3": hidden_col(a["L0_ffn_b3"], a["L0_ffn_sb3"]),
        "b2": np.pad(b2, ((WHOLE, 0), (0, 0))), "sel": np.tile(sel, (3, 1)),
    }
    nc = bacc.Bacc("TRN2", target_bir_lowering=False, num_devices=1)
    arrays = {"in_x": np.ascontiguousarray(a["L0_attn_x"])}
    x_d = nc.dram_tensor("in_x", [B, N, D], F32, kind="ExternalInput").ap()
    w_d = {}
    for name, v in w.items():
        arrays["in_" + name] = np.ascontiguousarray(v)
        w_d[name] = nc.dram_tensor("in_" + name, list(v.shape), F32, kind="ExternalInput").ap()
    out_d = nc.dram_tensor("out", [B, N, D], F32, kind="ExternalOutput").ap()
    parts_d = nc.dram_tensor("parts", [2, PAIRS, P, N], BF16, kind="Internal").ap()
    build_program(nc, x_d, w_d, parts_d, out_d)
    r = run(nc, [arrays], core_ids=[0])
    return r.results[0]["out"]
```

```python
from contextlib import ExitStack

import concourse.bass as bass
from concourse import mybir

F32 = mybir.dt.float32
BF16 = mybir.dt.bfloat16
U32 = mybir.dt.uint32
ALU = mybir.AluOpType
ACT = mybir.ActivationFunctionType
AX_X = mybir.AxisListType.X

P = 128
B, N, D = 8, 512, 128
NH, DH, TOP = 16, 8, 32
NQ = N // P
E, HID = 8, 176
FT = -(-(E + 1) * HID // P)
SCALE = DH ** -0.5
EPS = 1e-5
MASKED = -1e30
TAKEN = -1e38

QH, QL = 4, P // 4
NG = NH // QH
STEPS = 4
TILES = tuple((15 - 2 * s, 14 - 2 * s, 2 * s + 1, 2 * s) for s in range(STEPS))
KEYS = tuple(tuple(QL * (j + 1) for j in step) for step in TILES)
AT = tuple(tuple(sum(n[:k]) for k in range(4)) for n in KEYS)
COLS = sum(KEYS[0])
NC_ = 3
CHUNK_OF = (0, 1, 2, 2)
PS_AT = tuple((0, 512, 1024, 1024 + n[2]) for n in KEYS)
BLOCKS = tuple(tuple(j // 4 + 1 for j in step) for step in TILES)
BLOCK_AT = tuple(tuple(sum(n[:k]) for k in range(4)) for n in BLOCKS)
NB = sum(BLOCKS[0])
BLOCK_CHUNKS = tuple(((0, n[0]), (n[0], n[0] + n[1]), (n[0] + n[1], NB)) for n in BLOCKS)
SEARCHED = (3, 4, 4, 4)
PAIRS = 8
ROUNDS = TOP // 8


def search_count(s, r, replaced, k):
    n = SEARCHED[s]
    return (0 if r == 0 else 4 + n + 2 * n * (r - 1)) + ((4 if r == 0 else n) if replaced else 0) + k + 1


SEARCH = tuple(search_count(s, ROUNDS - 1, True, SEARCHED[s] - 1) for s in range(STEPS))


def before(counts, G, s):
    if s < 0:
        G, s = G - 1, s + STEPS
    return sum(counts) * G + sum(counts[:s])


ROUTE = 12
WHOLE = 32
FIRST_FFN = 6
VALUES_FIRST = (3, 4, FIRST_FFN + 1, FIRST_FFN + 2)
LATE = FT - (NH - FIRST_FFN)


def run(*parts):
    for _ in zip(*parts, strict=True):
        pass


def after(eng, sem, value):
    if isinstance(value, int) and value <= 0:
        return
    eng.wait_ge(sem, value)


def apart(eng, sem, value):
    after(eng, sem, value)
    if not isinstance(value, int):
        eng.nop(nofuse=True)


def build_program(nc, x_d, weights, parts_d, out_d):
    ctx = ExitStack()
    with ctx:
        def sb(name, shape, dt=F32):
            return ctx.enter_context(nc.sbuf_tensor(name, shape, dt))

        def ps(name, shape):
            return ctx.enter_context(nc.psum_tensor(name, shape, F32))

        def sem(name):
            return ctx.enter_context(nc.semaphore(name))

        W = {}
        for name, ap in weights.items():
            W[name] = sb("w_" + name, list(ap.shape))
        ident = W["ident"]
        identb = sb("identb", [P, P], BF16)
        cmaskb = sb("cmaskb", [P, QL], BF16)
        c_tanh = sb("c_tanh", [P, B])
        c_half = sb("c_half", [P, B])
        c_silu = sb("c_silu", [P, B])
        mod = sb("mod", [P, 6, B])
        g_sign = sb("g_sign", [P, 2, B])
        g_neg = sb("g_neg", [P, 2, B])
        bo_all = sb("bo_all", [P, 1])
        ga_bo = sb("ga_bo", [P, B])
        minus_half = sb("minus_half", [P, NQ])

        xin = sb("xin", [P, NQ, D])
        xres = sb("xres", [P, NQ, D])
        stats = sb("stats", [P, 2, NQ, 6])
        meanvar = sb("meanvar", [P, 2, NQ, 2])
        veps = sb("veps", [P, 2, NQ])
        rstd = sb("rstd", [P, 2, NQ])
        mrs = sb("mrs", [P, 2, NQ])
        nmr = sb("nmr", [P, 2, NQ])
        xn1 = sb("xn1", [P, NQ, D])
        xn2 = sb("xn2", [P, NQ, D])
        hT = sb("hT", [P, N])
        KQ = sb("KQ", [P, 2, N])
        PART = sb("PART", [P, 2, 3, N], BF16)
        KS = sb("KS", [P, NH // 2, N], BF16)
        QS = sb("QS", [P, NH // 2, N], BF16)
        QB = sb("QB", [P, 2, 2, N // QL, P], BF16)
        VX = sb("VX", [P, NQ, NH, DH + 1])
        S = sb("S", [P, STEPS, COLS])
        WORK = sb("WORK", [P, STEPS, COLS])
        TOPV = sb("TOPV", [P, STEPS, 4, TOP])
        NMAX = sb("NMAX", [P, STEPS, 4])
        E1 = sb("E1", [P, STEPS, NB * P])
        PT = sb("PT", [P, NB * P])
        OW = QH * (DH + 1)
        ORAW = sb("ORAW", [P, 2, 4 * STEPS, OW])
        rsum = sb("rsum", [P, 4 * STEPS])
        rown = sb("rown", [P, 4 * STEPS, QH])
        osb = sb("osb", [P, 4 * STEPS, D])
        OT = sb("OT", [P, N])
        yT = sb("yT", [P, N])
        x2 = sb("x2", [P, NQ, D])

        h2T = sb("h2T", [P, N])
        rmax = sb("rmax", [P, NQ])
        rdif = sb("rdif", [P, NQ, E])
        rexp = sb("rexp", [P, NQ, E])
        rs = sb("rs", [P, NQ])
        rinv = sb("rinv", [P, NQ])
        rscore = sb("rscore", [P, NQ, E])
        rbias = sb("rbias", [P, NQ, E])
        rtop = sb("rtop", [P, NQ, 8])
        ridx = sb("ridx", [P, NQ, 8], U32)
        ridf = sb("ridf", [P, NQ, 2])
        rhit = sb("rhit", [P, 2, NQ, E])
        rw = sb("rw", [P, NQ, P])
        rhb = sb("rhb", [P, 2, NQ, E], BF16)
        rrem = sb("rrem", [P, NQ, E])
        rwT = sb("rwT", [WHOLE + E + 1, N])
        rwTb = sb("rwTb", [3 * (E + 1), N], BF16)
        selb = sb("selb", [3 * (E + 1), FT * P], BF16)
        fa = sb("fa", [P, 2, N])
        fc = sb("fc", [P, 2, N])
        ft = sb("ft", [P, 2, N])
        fr = sb("fr", [P, 2, N])
        fh = sb("fh", [P, 2, N])
        zT = sb("zT", [P, N])
        osum = sb("osum", [P, NQ, D])

        pS = ps("pS", [P, NC_ * 512])
        pT = ps("pT", [P, 512])
        F0 = ps("F0", [P, 512])
        F1 = ps("F1", [P, 512])
        pY = ps("pY", [P, 512])
        pO = ps("pO", [P, 512])
        names = """w_loaded ffn_loaded xin_loaded xres_loaded stored const_ready vx_ones rw_ready setup_act setup_dve
            setup_pe scores scopied nmax_done e1_done e2_done search p_done pt_full pt_evac pv_done o_evac
            zeroed spread k_full q_full k_evac q_evac k_split q_split split_k split_q parts_stored rsplit
            sel_ready v_full v_evac bn1 rstd1 ln1_done ln1T_full hT_done norm_done OT_full OT_evac wo_full
            yT_done att_full res_done bn2 rstd2 ln2_done ln2T_full h2T_done log_full rsub_done rexp_done route
            rw_done rwT_full rwT_done up1_full up3_full gate_full a_done c_done u_done t_done t1_done r_done
            v_done h_done w2_done y_full z_done zT_full fin_done tail_up1 tail_up3 tail_gate tail_down tail_a
            tail_u tail_t tail_g tail_h norm_step sub_step stat_step rsqrt1_step rsqrt2_step rsum_done"""
        s = {n: sem("s_" + n) for n in names.split()}
        stacked = [sem(f"s_stacked{hp}") for hp in range(NH // 2)]

        act_names = ("cT", "wmod", "wkT", "bk", "woT", "bo", "rows")
        TAIL = [(B - 2, t) for t in range(FT - LATE, FT)] + [(B - 1, t) for t in range(FT)]
        up1_bank = (pS[:, 0:512], pS[:, 512:1024])
        up3_bank = (pS[:, 1024:1536], pT[:, :])
        ffn_names = ("w1", "w3", "w2", "sel", "b1", "b3", "b2", "gwT", "gb", "iota")
        block = ctx.enter_context(nc.Block())

        def xrows(d, b):
            return d[bass.ds(b, 1), :, :].rearrange("o (q p) d -> p (o q) d", p=P)

        @block.sync
        def _(sp):
            def load_x(b):
                after(sp, s["ln1_done"], b)
                sp.dma_start(xin[:, :, :], xrows(x_d, b)).then_inc(s["xin_loaded"], 16)

            def load_xres(b):
                after(sp, s["res_done"], b)
                sp.dma_start(xres[:, :, :], xrows(x_d, b)).then_inc(s["xres_loaded"], 16)

            def store(b):
                sp.wait_ge(s["fin_done"], b + 1)
                sp.dma_start(xrows(out_d, b), osum[:, :, :]).then_inc(s["stored"], 16)

            def store_parts(bb):
                for hp in range(NH // 2):
                    after(sp, stacked[hp], 64 * bb)
                for side, split in enumerate(("k_split", "q_split")):
                    sp.wait_ge(s[split], bb + 1)
                    for a in range(3):
                        n = min(3, PAIRS - 3 * a)
                        src = PART[:, side, 0:n, :] if side == 0 else \
                            PART[:, side, a:a + 1, :].to_broadcast([P, n, N])
                        sp.dma_start(parts_d[side, 3 * a:3 * a + n, :, :].rearrange("t p n -> p t n"), src)\
                            .then_inc(s["parts_stored"], 16)
                apart(sp, s["parts_stored"], 96 * (bb + 1))

            def load_stacks(bb):
                for hp in range(NH // 2):
                    after(sp, s["scores"], NC_ * (NH * (bb - 1) + QH * (hp // 2) + STEPS))
                    for side, dst in enumerate((KS, QS)):
                        for e in range(2):
                            rows = DH * (2 * hp + e)
                            sp.dma_start(dst[64 * e:64 * e + 64, hp, :], parts_d[side, :, rows:rows + DH, :])\
                                .then_inc(stacked[hp], 16)

            def batch(b, old, next_x, prep):
                if old:
                    store(b - 2)
                load_xres(b)
                if next_x:
                    load_x(b + 2)
                if prep:
                    store_parts(b + 1)
                    load_stacks(b + 1)

            load_x(0)
            for name in weights:
                if name not in ffn_names and name not in act_names:
                    sp.dma_start(W[name][:, :], weights[name]).then_inc(s["w_loaded"], 16)
            load_x(1)
            for name in ffn_names[:1]:
                sp.dma_start(W[name][:, :], weights[name]).then_inc(s["ffn_loaded"], 16)
            store_parts(0)
            load_stacks(0)
            for name in ffn_names[1:]:
                sp.dma_start(W[name][:, :], weights[name]).then_inc(s["ffn_loaded"], 16)
            batch(0, False, True, True)
            batch(1, False, True, True)
            with sp.Fori(2, B - 2) as b:
                batch(b, True, True, True)
            batch(B - 2, True, False, True)
            batch(B - 1, True, False, False)
            store(B - 2)
            store(B - 1)
            sp.wait_ge(s["stored"], 16 * B)

        n_attn_loads = 16 * (len(weights) - len(ffn_names))
        n_ffn_loads = 16 * len(ffn_names)

        def split(eng, bb, side):
            evac, step, done = (("k_evac", "split_k", "k_split"), ("q_evac", "split_q", "q_split"))[side]
            eng.wait_ge(s[evac], bb + 1)
            eng.tensor_tensor(KQ[:, side, :], KQ[:, side, :], PART[:, side, 0, :], ALU.subtract).then_inc(s[step], 1)
            apart(eng, s[step], 2 * bb + 1)
            eng.tensor_copy(PART[:, side, 1, :], KQ[:, side, :]).then_inc(s[step], 1)
            eng.wait_ge(s[step], 2 * bb + 2)
            eng.tensor_tensor(PART[:, side, 2, :], KQ[:, side, :], PART[:, side, 1, :], ALU.subtract)\
                .then_inc(s[done], 1)

        @block.gpsimd
        def _(pool):
            pool.memset(minus_half[:, :], -0.5).then_inc(s["const_ready"], 1)
            for g in range(2):
                for p in range(2):
                    own = QL * 2 * (1 - p)
                    pool.memset(QB[:, g, p, :, own:own + 2 * QL], 0.0).then_inc(s["const_ready"], 1)
            pool.memset(VX[:, :, :, :], 1.0).then_inc(s["vx_ones"], 1)
            pool.memset(rw[:, :, :], 0.0).then_inc(s["rw_ready"], 1)
            pool.wait_ge(s["rw_ready"], 1)
            pool.memset(rw[:, :, E:E + 1], 1.0).then_inc(s["rw_ready"], 1)
            pool.memset(rw[:, :, WHOLE + E:WHOLE + E + 1], 1.0).then_inc(s["rw_ready"], 1)
            pool.wait_ge(s["w_loaded"], n_attn_loads)
            pool.tensor_copy(identb[:, :], ident[:, :]).then_inc(s["const_ready"], 1)
            pool.tensor_copy(cmaskb[:, :], W["cmask"][:, :]).then_inc(s["const_ready"], 1)

            def rsqrt(ln, bb):
                bn, step, done = (("bn1", "rsqrt1_step", "rstd1"), ("bn2", "rsqrt2_step", "rstd2"))[ln]
                apart(pool, s[bn], bb + 1)
                pool.tensor_scalar(veps[:, ln, :], meanvar[:, ln, :, 1], EPS, 1.0, ALU.add, ALU.mult).then_inc(s[step], 1)
                pool.wait_ge(s[step], 3 * bb + 1)
                pool.tensor_tensor(rstd[:, ln, :], veps[:, ln, :], minus_half[:, :], ALU.pow).then_inc(s[step], 1)
                pool.wait_ge(s[step], 3 * bb + 2)
                pool.tensor_tensor(mrs[:, ln, :], meanvar[:, ln, :, 0], rstd[:, ln, :], ALU.mult).then_inc(s[step], 1)
                apart(pool, s[step], 3 * bb + 3)
                pool.tensor_scalar(nmr[:, ln, :], mrs[:, ln, :], -1.0, 1.0, ALU.mult, ALU.mult).then_inc(s[done], 1)

            def neg_max(G, st):
                apart(pool, s["search"], before(SEARCH, G, st) + search_count(st, 0, False, 3))
                pool.tensor_scalar(NMAX[:, st, :], TOPV[:, st, :, 0], -SCALE, 1.0, ALU.mult,
                                   ALU.mult).then_inc(s["nmax_done"], 1)

            def normalise(b, g):
                G = NG * b + g
                pool.wait_ge(s["rsum_done"], G + 1)
                pool.tensor_tensor(rown[:, :, :], rsum[:, :].unsqueeze(2).to_broadcast([P, 4 * STEPS, QH]),
                                   W["own"][:, :].unsqueeze(1).to_broadcast([P, 4 * STEPS, QH]),
                                   ALU.mult).then_inc(s["norm_step"], 1)
                after(pool, s["OT_full"], b)
                pool.wait_ge(s["norm_step"], G + 1)
                pool.tensor_tensor(osb[:, :, QH * DH * g:QH * DH * (g + 1)].rearrange("p k (e d) -> p k e d", e=QH),
                                   ORAW[:, g % 2, :, :].rearrange("p k (e c) -> p k e c", e=QH)[:, :, :, 0:DH],
                                   rown[:, :, :].unsqueeze(3).to_broadcast([P, 4 * STEPS, QH, DH]),
                                   ALU.mult).then_inc(s["norm_done"], 1)

            def split_weights(b):
                whole = rw[:, :, WHOLE:WHOLE + E]
                apart(pool, s["rw_done"], b + 1)
                steps = (lambda: pool.tensor_copy(rhb[:, 0, :, :], whole),
                         lambda: pool.tensor_copy(rw[:, :, 0:E], rhb[:, 0, :, :]),
                         lambda: pool.tensor_tensor(rrem[:, :, :], whole, rhb[:, 0, :, :], ALU.subtract),
                         lambda: pool.tensor_copy(rhb[:, 1, :, :], rrem[:, :, :]),
                         lambda: pool.tensor_copy(rw[:, :, E + 1:2 * E + 1], rhb[:, 1, :, :]),
                         lambda: pool.tensor_tensor(rw[:, :, 2 * E + 2:3 * E + 2], rrem[:, :, :], rhb[:, 1, :, :],
                                                    ALU.subtract))
                for i, step in enumerate(steps):
                    if i:
                        apart(pool, s["rsplit"], len(steps) * b + i)
                    step().then_inc(s["rsplit"], 1)

            def keep_selected(G, st):
                for k in range(SEARCHED[st]):
                    n, at, to = KEYS[st][k], AT[st][k], P * BLOCK_AT[st][k]
                    pool.wait_ge(s["e2_done"], before(SEARCHED, G, st) + k + 1)
                    pool.tensor_tensor(E1[:, st, to:to + n], E1[:, st, to:to + n], WORK[:, st, at:at + n],
                                       ALU.subtract).then_inc(s["p_done"], 1)

            def linear_product(T, tp):
                pool.wait_ge(s["c_done"], T + 1)
                pool.tensor_tensor(fa[:, tp, :], fa[:, tp, :], fc[:, tp, :], ALU.mult).then_inc(s["u_done"], 1)

            def weigh(T, tp):
                apart(pool, s["t_done"], T + 1)
                pool.tensor_scalar(ft[:, tp, :], ft[:, tp, :], 1.0, 1.0, ALU.add, ALU.mult).then_inc(s["t1_done"], 1)
                pool.wait_ge(s["r_done"], T + 1)
                pool.tensor_tensor(fa[:, tp, :], fa[:, tp, :], fr[:, tp, :], ALU.mult).then_inc(s["v_done"], 1)
                pool.wait_ge(s["v_done"], T + 1)
                pool.tensor_tensor(fh[:, tp, :], fa[:, tp, :], ft[:, tp, :], ALU.mult).then_inc(s["h_done"], 1)

            def expert_tile(b, t):
                T = FT * b + t
                if t > 1:
                    weigh(T - 1, (t - 1) % 2)
                if t < FT:
                    linear_product(T, t % 2)

            def batch(b, prep, ffn, old):
                for h in range(NH):
                    g, st = h // STEPS, h % STEPS
                    G = NG * b + g
                    neg_max(G, st)
                    if prep and h == 1:
                        rsqrt(0, b + 1)
                    if prep and h == 5:
                        split(pool, b + 1, 0)
                    if ffn and h == 5:
                        rsqrt(1, b - 1)
                    if prep and h == 5:
                        split(pool, b + 1, 1)
                    if ffn and h == FIRST_FFN + 1:
                        split_weights(b - 1)
                    if ffn and h >= FIRST_FFN:
                        expert_tile(b - 1, h - FIRST_FFN)
                    elif old and h <= LATE:
                        expert_tile(b - 2, FT - LATE + h)
                    if st == 2 and g:
                        normalise(b, g - 1)
                    elif h == 1 and ffn:
                        normalise(b - 1, NG - 1)
                    if ffn and h == FIRST_FFN + 1:
                        weigh(FT * (b - 1), 0)
                    keep_selected(G, st)
                    if not ffn and h == NH // 2:
                        pool.wait_ge(s["ffn_loaded"], n_ffn_loads)
                        pool.tensor_copy(selb[:, :], W["sel"][:, :]).then_inc(s["sel_ready"], 1)

            pool.wait_ge(s["const_ready"], 7)
            rsqrt(0, 0)
            batch(0, True, False, False)
            batch(1, True, True, False)
            with pool.Fori(2, B - 1) as b:
                batch(b, True, True, True)
            batch(B - 1, False, True, True)
            weigh(FT * (B - 1) - LATE - 1, (FT - LATE - 1) % 2)
            normalise(B - 1, NG - 1)
            rsqrt(1, B - 1)
            split_weights(B - 1)

        @block.vector
        def _(dve):
            def step(b, g, st, between):
                G, n_search = NG * b + g, SEARCHED[st]
                H = STEPS * G + st
                start = before(SEARCH, G, st)
                for r in range(ROUNDS):
                    src = WORK if r else S
                    for k in range(n_search if r else 4):
                        n, at = KEYS[st][k], AT[st][k]
                        if r == 0:
                            if k == 0:
                                apart(dve, s["nmax_done"], H - 3)
                            apart(dve, s["scopied"], NC_ * H + CHUNK_OF[k] + 1)
                        else:
                            apart(dve, s["search"], start + search_count(st, r - 1, True, k))
                        dve.max(TOPV[:, st, k, 8 * r:8 * r + 8], src[:, st, at:at + n]).then_inc(s["search"], 1)
                    for k in range(n_search):
                        n, at = KEYS[st][k], AT[st][k]
                        if r == 0 and k == 0:
                            apart(dve, s["p_done"], before(SEARCHED, G, st - 3))
                        apart(dve, s["search"], start + search_count(st, r, False, k))
                        dve.match_replace(out=WORK[:, st, at:at + n], in_to_replace=TOPV[:, st, k, 8 * r:8 * r + 8],
                                          in_values=src[:, st, at:at + n], imm_value=TAKEN).then_inc(s["search"], 1)
                    between(r)

            def statistics(ln, src, bb, done):
                step_sem = s["stat_step"] if ln == 0 else s["sub_step"]
                for q in range(NQ):
                    dve.bn_stats(stats[:, ln, q, :], src[:, q, :]).then_inc(step_sem, 1)
                for q in range(NQ):
                    apart(dve, step_sem, 4 * bb + q + 1)
                    last = dve.bn_aggr(meanvar[:, ln, q, :], stats[:, ln, q, :])
                last.then_inc(s[done], 1)

            def invert_sums(b, g):
                G = NG * b + g
                dve.wait_ge(s["o_evac"], STEPS * (G + 1))
                after(dve, s["norm_done"], G)
                dve.reciprocal(rsum[:, :], ORAW[:, g % 2, :, DH]).then_inc(s["rsum_done"], 1)

            def finish(fb, x2=x2):
                dve.wait_ge(s["zT_full"], fb + 1)
                after(dve, s["stored"], 16 * fb)
                dve.tensor_tensor(osum[:, :, :], x2[:, :, :], pY[:, :].rearrange("p (q d) -> p q d", q=NQ),
                                  ALU.add).then_inc(s["fin_done"], 1)

            def residual(b, x2=x2):
                dve.wait_ge(s["att_full"], b + 1)
                dve.wait_ge(s["xres_loaded"], 16 * (b + 1))
                if not (isinstance(b, int) and b == B - 1):
                    after(dve, s["fin_done"], b)
                dve.tensor_tensor(x2[:, :, :], xres[:, :, :], F0[:, :].rearrange("p (q d) -> p q d", q=NQ),
                                  ALU.add).then_inc(s["res_done"], 1)
                apart(dve, s["res_done"], b + 1)
                statistics(1, x2, b, "bn2")

            def logits_minus_max(b):
                logits = F1[:, 0:NQ * E].rearrange("p (q e) -> p q e", q=NQ)
                dve.wait_ge(s["log_full"], b + 1)
                dve.tensor_reduce(rmax[:, :], logits, AX_X, ALU.max).then_inc(s["route"], 1)
                dve.wait_ge(s["route"], ROUTE * b + 1)
                dve.tensor_tensor(rdif[:, :, :], logits, rmax[:, :].unsqueeze(2).to_broadcast([P, NQ, E]),
                                  ALU.subtract).then_inc(s["rsub_done"], 1)

            def routing(b):
                at = [ROUTE * b + 1]

                def link_step(ins):
                    ins.then_inc(s["route"], 1)
                    at[0] = at[0] + 1

                def settle():
                    apart(dve, s["route"], at[0])

                dve.wait_ge(s["rexp_done"], b + 1)
                dve.wait_ge(s["ffn_loaded"], n_ffn_loads)
                link_step(dve.tensor_reduce(rs[:, :], rexp[:, :, :], AX_X, ALU.add))
                settle()
                link_step(dve.reciprocal(rinv[:, :], rs[:, :]))
                settle()
                link_step(dve.tensor_tensor(rscore[:, :, :], rexp[:, :, :],
                                       rinv[:, :].unsqueeze(2).to_broadcast([P, NQ, E]), ALU.mult))
                settle()
                link_step(dve.tensor_tensor(rbias[:, :, :], rscore[:, :, :],
                                       W["gb"][:, :].unsqueeze(1).to_broadcast([P, NQ, E]), ALU.add))
                settle()
                for q in range(NQ):
                    ins = dve.max(rtop[:, q, :], rbias[:, q, :])
                link_step(ins)
                settle()
                for q in range(NQ):
                    ins = dve.max_index(ridx[:, q, :], rtop[:, q, :], rbias[:, q, :])
                link_step(ins)
                settle()
                link_step(dve.tensor_copy(ridf[:, :, :], ridx[:, :, 0:2]))
                settle()
                for i in range(2):
                    link_step(dve.tensor_tensor(rhit[:, i, :, :], ridf[:, :, i:i + 1].to_broadcast([P, NQ, E]),
                                           W["iota"][:, :].unsqueeze(1).to_broadcast([P, NQ, E]), ALU.is_equal))
                settle()
                link_step(dve.tensor_tensor(rhit[:, 0, :, :], rhit[:, 0, :, :], rhit[:, 1, :, :], ALU.add))
                settle()
                link_step(dve.tensor_tensor(rdif[:, :, :], rhit[:, 0, :, :], rscore[:, :, :], ALU.mult))
                settle()
                after(dve, s["rwT_full"], b)
                if not isinstance(b, int) or b == 0:
                    dve.wait_ge(s["rw_ready"], 3)
                dve.tensor_copy(rw[:, :, WHOLE:WHOLE + E], rdif[:, :, :]).then_inc(s["rw_done"], 1)

            def batch(b, prep, ffn, old):
                for h in range(NH):
                    g, st = h // STEPS, h % STEPS

                    def others(r):
                        if h == 0 and r == 3 and prep:
                            dve.wait_ge(s["xin_loaded"], 16 * (b + 2))
                            statistics(0, xin, b + 1, "bn1")
                        if h == 1 and r == 3 and ffn:
                            invert_sums(b - 1, NG - 1)
                        if st == 2 and r == 1 and g:
                            invert_sums(b, g - 1)
                        if h == 5 and r == 3 and old:
                            finish(b - 2)
                        if ffn:
                            if h == 5 and r == 3:
                                residual(b - 1)
                            elif h == 7 and r == 0:
                                logits_minus_max(b - 1)
                            elif h == 7 and r == 2:
                                routing(b - 1)

                    step(b, g, st, others)

            at = [0]

            def link(ins):
                at[0] += 1
                ins.then_inc(s["setup_dve"], 1)
                dve.wait_ge(s["setup_dve"], at[0])

            dve.memset(E1[:, :, :], 0.0).then_inc(s["zeroed"], 1)
            dve.wait_ge(s["xin_loaded"], 16)
            statistics(0, xin, 0, "bn1")
            dve.wait_ge(s["setup_act"], 1)
            link(dve.tensor_scalar(c_half[:, :], W["cT"][:, :], 0.5, None, ALU.mult))
            link(dve.scalar_tensor_tensor(out=c_silu[:, :], in0=c_tanh[:, :], scalar=1.0, in1=c_half[:, :],
                                          op0=ALU.add, op1=ALU.mult))
            dve.wait_ge(s["setup_pe"], 1)
            link(dve.tensor_copy(mod[:, :, :], F0[:, 0:6 * B].rearrange("p (m b) -> p m b", m=6)))
            link(dve.tensor_tensor(bo_all[:, :], W["bo"][:, :], F0[:, 6 * B:6 * B + 1], ALU.add))
            for i in (1, 4):
                link(dve.tensor_scalar(mod[:, i, :], mod[:, i, :], 1.0, None, ALU.add))
            for i, m in enumerate((2, 5)):
                link(dve.tensor_scalar(g_sign[:, i, :], mod[:, m, :], 0.0, 2.0, ALU.is_ge, ALU.mult))
                link(dve.tensor_scalar(g_sign[:, i, :], g_sign[:, i, :], -1.0, None, ALU.add))
                link(dve.tensor_scalar(g_neg[:, i, :], mod[:, m, :], -1.0, 0.25, ALU.mult, ALU.max))
                link(dve.tensor_tensor(g_neg[:, i, :], g_neg[:, i, :], mod[:, m, :], ALU.max))
                link(dve.tensor_tensor(mod[:, m, :], g_neg[:, i, :], g_sign[:, i, :], ALU.mult))
            link(dve.tensor_tensor(ga_bo[:, :], mod[:, 2, :], bo_all[:, :].to_broadcast([P, B]), ALU.mult))
            assert at[0] == SETUP_DVE
            split(dve, 0, 0)
            split(dve, 0, 1)

            batch(0, True, False, False)
            batch(1, True, True, False)
            with dve.Fori(2, B - 1) as b:
                batch(b, True, True, True)
            batch(B - 1, False, True, True)

            def tail_product(n):
                dve.wait_ge(s["tail_up3"], n + 1)
                after(dve, s["tail_t"], n - 1)
                after(dve, s["tail_g"], n - 1)
                dve.wait_ge(s["tail_a"], n + 1)
                t = TAIL[n][1]
                dve.scalar_tensor_tensor(out=fc[:, n % 2, :], in0=up3_bank[n % 2], scalar=W["b3"][:, t:t + 1],
                                         in1=fa[:, n % 2, :], op0=ALU.add, op1=ALU.mult).then_inc(s["tail_u"], 1)

            def tail_silu(n):
                dve.wait_ge(s["tail_t"], n + 1)
                after(dve, s["tail_h"], n - 1)
                dve.scalar_tensor_tensor(out=fr[:, n % 2, :], in0=ft[:, n % 2, :], scalar=1.0, in1=fc[:, n % 2, :],
                                         op0=ALU.add, op1=ALU.mult).then_inc(s["tail_g"], 1)
                dve.wait_ge(s["tail_g"], n + 1)
                dve.wait_ge(s["tail_gate"], n + 1)
                if n < 2:
                    dve.wait_ge(s["w2_done"], FT * (B - 1) - LATE - 1 + n)
                else:
                    dve.wait_ge(s["tail_down"], n - 1)
                dve.tensor_tensor(fh[:, n % 2, :], fr[:, n % 2, :], pO[:, :], ALU.mult).then_inc(s["tail_h"], 1)

            invert_sums(B - 1, NG - 1)
            tail_product(0)
            tail_product(1)
            tail_silu(0)
            tail_silu(1)
            tail_product(2)
            residual(B - 1, xin)
            tail_silu(2)
            logits_minus_max(B - 1)
            finish(B - 2)
            routing(B - 1)
            for n in range(LATE, len(TAIL)):
                if n == LATE:
                    tail_product(n)
                    tail_product(n + 1)
                tail_silu(n)
                if n + 2 < len(TAIL):
                    tail_product(n + 2)
            finish(B - 1, xin)

        @block.scalar
        def _(act):
            def copy_scores(G, st):
                if st >= STEPS:
                    G, st = G + 1, st - STEPS
                H = STEPS * G + st
                for i in range(NC_):
                    act.wait_ge(s["scores"], NC_ * H + i + 1)
                    if i == 0:
                        after(act, s["search"], before(SEARCH, G - 1, st) + search_count(st, 0, True, SEARCHED[st] - 1))
                        after(act, s["e1_done"], 4 * (H - 3))
                    at, n = AT[st][i], COLS - AT[st][i] if i == 2 else KEYS[st][i]
                    act.activation(S[:, st, at:at + n], pS[:, 512 * i:512 * i + n], ACT.Copy).then_inc(s["scopied"], 1)

            def exp_all(G, st):
                H = STEPS * G + st
                act.wait_ge(s["nmax_done"], H + 1)
                after(act, s["pt_full"], NC_ * (H - 3))
                for k in range(4):
                    n, at, to = KEYS[st][k], AT[st][k], P * BLOCK_AT[st][k]
                    act.activation(E1[:, st, to:to + n], S[:, st, at:at + n], ACT.Exp,
                                   bias=NMAX[:, st, k:k + 1], scale=SCALE).then_inc(s["e1_done"], 1)

            def exp_rest(G, st):
                for k in range(SEARCHED[st]):
                    n, at = KEYS[st][k], AT[st][k]
                    act.wait_ge(s["search"], before(SEARCH, G, st) + search_count(st, ROUNDS - 1, True, k))
                    act.activation(WORK[:, st, at:at + n], WORK[:, st, at:at + n], ACT.Exp,
                                   bias=NMAX[:, st, k:k + 1], scale=SCALE).then_inc(s["e2_done"], 1)

            def evacuate_chunk(G, st, i):
                if st < 0:
                    G, st = G - 1, st + STEPS
                H = STEPS * G + st
                lo, hi = (P * n for n in BLOCK_CHUNKS[st][i])
                act.wait_ge(s["pt_full"], NC_ * H + i + 1)
                if i == 0:
                    after(act, s["pv_done"], H)
                act.activation(PT[:, lo:hi], pT[:, 0:hi - lo], ACT.Copy).then_inc(s["pt_evac"], 1)

            def spread(G, g, bb, st):
                for piece in ((0, 1), (2, 3), (), ())[st]:
                    p, e = piece // 2, piece % 2
                    own = QL * (2 * p + e)
                    if e == 0:
                        act.wait_ge(stacked[2 * g + p], 64 * (bb + 1))
                    after(act, s["scores"], NC_ * STEPS * (G - 1))
                    act.activation(QB[:, g % 2, p, :, own:own + QL],
                                   QS[:, 2 * g + p, :].rearrange("r (j c) -> r j c", c=QL), ACT.Copy,
                                   scale=W["rows"][:, e:e + 1]).then_inc(s["spread"], 1)

            def evacuate_outputs(G, g, st):
                if st < 0:
                    G, g, st = G - 1, g - 1, st + STEPS
                act.wait_ge(s["pv_done"], STEPS * G + st + 1)
                after(act, s["norm_done"], G - 1)
                act.activation(ORAW[:, g % 2, 4 * st:4 * st + 4, :], pO[:, 0:4 * OW].rearrange("p (k c) -> p k c", k=4),
                               ACT.Copy).then_inc(s["o_evac"], 1)

            def linear_1(T, t, tp):
                act.wait_ge(s["up1_full"], T + 1)
                act.activation(fa[:, tp, :], F0[:, :], ACT.Identity, bias=W["b1"][:, bass.ds(t, 1)])\
                    .then_inc(s["a_done"], 1)

            def linear_3(T, t, tp):
                act.wait_ge(s["up3_full"], T + 1)
                act.activation(fc[:, tp, :], F1[:, :], ACT.Identity, bias=W["b3"][:, bass.ds(t, 1)])\
                    .then_inc(s["c_done"], 1)

            def half_tanh(T, tp):
                act.wait_ge(s["u_done"], T + 1)
                act.activation(ft[:, tp, :], fa[:, tp, :], ACT.Tanh, scale=0.5).then_inc(s["t_done"], 1)

            def expert_weights(T, tp):
                act.wait_ge(s["gate_full"], T + 1)
                act.activation(fr[:, tp, :], F0[:, :], ACT.Copy).then_inc(s["r_done"], 1)

            def layer_norm(ln, src, dst, bb, rstd_sem, done):
                act.wait_ge(s[rstd_sem], bb + 1)
                for q in range(NQ):
                    ins = act.activation(dst[:, q, :], src[:, q, :], ACT.Identity, bias=nmr[:, ln, q:q + 1],
                                         scale=rstd[:, ln, q:q + 1])
                ins.then_inc(s[done], 1)

            def modulate_1(bb, bank):
                act.wait_ge(s["ln1T_full"], bb + 1)
                after(act, s["v_full"], bb)
                act.activation(hT[:, :], bank[:, :], ACT.Identity, bias=mod[:, 0, bass.ds(bb, 1)],
                               scale=mod[:, 1, bass.ds(bb, 1)]).then_inc(s["hT_done"], 1)

            def evacuate_kq(bb, side, bank):
                full, bias, done = (("k_full", "bk", "k_evac"), ("q_full", "bq", "q_evac"))[side]
                act.wait_ge(s[full], bb + 1)
                after(act, s["parts_stored"], 96 * bb)
                act.activation(KQ[:, side, :], bank[:, :], ACT.Identity, bias=W[bias][:, 0:1])
                act.activation(PART[:, side, 0, :], bank[:, :], ACT.Identity, bias=W[bias][:, 0:1])\
                    .then_inc(s[done], 1)

            def evacuate_v(bb):
                act.wait_ge(s["v_full"], bb + 1)
                after(act, s["pv_done"], NH * bb)
                act.activation(VX[:, :, :, 0:DH], F0[:, :].rearrange("p (q h d) -> p q h d", q=NQ, d=DH),
                               ACT.Copy).then_inc(s["v_evac"], 1)

            def evacuate_OT(b):
                act.wait_ge(s["OT_full"], b + 1)
                act.activation(OT[:, :], F1[:, :], ACT.Copy).then_inc(s["OT_evac"], 1)

            def gate_attention(b):
                act.wait_ge(s["wo_full"], b + 1)
                act.activation(yT[:, :], F1[:, :], ACT.Identity, bias=ga_bo[:, bass.ds(b, 1)],
                               scale=mod[:, 2, bass.ds(b, 1)]).then_inc(s["yT_done"], 1)

            def modulate_2(b):
                act.wait_ge(s["ln2T_full"], b + 1)
                act.activation(h2T[:, :], F0[:, :], ACT.Identity, bias=mod[:, 3, bass.ds(b, 1)],
                               scale=mod[:, 4, bass.ds(b, 1)]).then_inc(s["h2T_done"], 1)

            def router_exp(b):
                act.wait_ge(s["rsub_done"], b + 1)
                act.activation(rexp[:, :, :], rdif[:, :, :], ACT.Exp).then_inc(s["rexp_done"], 1)

            def route_rows(b):
                act.wait_ge(s["rwT_full"], b + 1)
                act.activation(rwTb[:, :], F0[0:3 * (E + 1), :], ACT.Copy)
                act.activation(rwT[WHOLE:WHOLE + E + 1, :], F0[WHOLE:WHOLE + E + 1, :], ACT.Copy)\
                    .then_inc(s["rwT_done"], 1)

            def gate_experts(b):
                act.wait_ge(s["y_full"], b + 1)
                act.activation(zT[:, :], pY[:, :], ACT.Copy, scale=mod[:, 5, bass.ds(b, 1)]).then_inc(s["z_done"], 1)

            def probs(G, g, st):
                for i in range(NC_):
                    evacuate_chunk(G, st, i)
                    yield
                evacuate_outputs(G, g, st)
                yield

            def expert_tile(b, t):
                T, tp = FT * b + t, t % 2
                if t > 1:
                    expert_weights(T - 1, 1 - tp)
                if t != 1:
                    yield
                if t < FT:
                    linear_1(T, t, tp)
                yield
                if t < FT:
                    linear_3(T, t, tp)
                yield
                if t == 0:
                    router_exp(b)
                if t == 1:
                    route_rows(b)
                    yield
                    expert_weights(T - 1, 1 - tp)
                if t < FT:
                    half_tanh(T, tp)
                yield

            def next_kq(bb, k_bank, q_bank):
                modulate_1(bb, q_bank)
                yield
                evacuate_kq(bb, 0, k_bank)
                yield
                evacuate_kq(bb, 1, q_bank)
                yield
                yield

            def attention_out(b):
                evacuate_OT(b)
                yield
                gate_attention(b)
                yield
                yield
                yield

            def norm_2(b, x2=x2):
                layer_norm(1, x2, xn2, b, "rstd2", "ln2_done")
                modulate_2(b)

            def experts_out(b):
                gate_experts(b)
                yield
                yield
                yield
                yield

            def search_exps(G, st):
                yield
                exp_all(G, st)
                yield
                yield
                yield

            def batch(b, prep, ffn, old):
                for h in range(NH):
                    g, st = h // STEPS, h % STEPS
                    G = NG * b + g
                    if h < NH - 2 or prep:
                        copy_scores(G, st + 2)
                    beside = []
                    if old and h <= LATE:
                        beside.append(expert_tile(b - 2, FT - LATE + h))
                    if prep and h == 3:
                        layer_norm(0, xin, xn1, b + 1, "rstd1", "ln1_done")
                    if ffn and h == 3:
                        beside.append(attention_out(b - 1))
                    if old and h == 4:
                        beside.append(experts_out(b - 2))
                    if prep and h == 4:
                        beside.append(next_kq(b + 1, F1, F1))
                    if ffn and h >= FIRST_FFN:
                        beside.append(expert_tile(b - 1, h - FIRST_FFN))
                    if h or ffn:
                        beside.insert(0 if h in VALUES_FIRST else len(beside), probs(G, g, st - 1))
                    beside.append(search_exps(G, st))
                    run(*beside)
                    if ffn and h == 5:
                        norm_2(b - 1)
                    if h == 0:
                        evacuate_v(b)
                    if g < NG - 1:
                        spread(G + 1, g + 1, b, st)
                    elif prep:
                        spread(G + 1, 0, b + 1, st)
                    exp_rest(G, st)

            for name in act_names:
                act.dma_start(W[name][:, :], weights[name]).then_inc(s["w_loaded"], 16)
            act.wait_ge(s["w_loaded"], n_attn_loads)
            act.activation(c_tanh[:, :], W["cT"][:, :], ACT.Tanh, scale=0.5).then_inc(s["setup_act"], 1)
            layer_norm(0, xin, xn1, 0, "rstd1", "ln1_done")
            act.wait_ge(s["setup_dve"], SETUP_DVE)
            modulate_1(0, F1)
            evacuate_kq(0, 0, F0)
            evacuate_kq(0, 1, F1)
            act.wait_ge(s["const_ready"], 5)
            for st in range(STEPS):
                spread(0, 0, 0, st)
            copy_scores(0, 0)
            copy_scores(0, 1)
            act.wait_ge(s["vx_ones"], 1)
            act.wait_ge(s["zeroed"], 1)
            batch(0, True, False, False)
            act.wait_ge(s["ffn_loaded"], n_ffn_loads)
            batch(1, True, True, False)
            with act.Fori(2, B - 1) as b:
                batch(b, True, True, True)
            batch(B - 1, False, True, True)

            def tail_linear(n):
                act.wait_ge(s["tail_up1"], n + 1)
                if n < 2:
                    act.wait_ge(s["h_done"], FT * (B - 1) - LATE - 1 + n)
                else:
                    act.wait_ge(s["tail_u"], n - 1)
                t = TAIL[n][1]
                act.activation(fa[:, n % 2, :], up1_bank[n % 2], ACT.Identity, bias=W["b1"][:, t:t + 1])\
                    .then_inc(s["tail_a"], 1)

            def tail_tanh(n):
                act.wait_ge(s["tail_u"], n + 1)
                after(act, s["tail_g"], n - 1)
                act.activation(ft[:, n % 2, :], fc[:, n % 2, :], ACT.Tanh, scale=0.5).then_inc(s["tail_t"], 1)

            expert_weights(FT * (B - 1) - LATE - 1, (FT - LATE - 1) % 2)
            run(probs(NG * B, 0, -1))
            tail_linear(0)
            tail_linear(1)
            tail_tanh(0)
            evacuate_OT(B - 1)
            tail_tanh(1)
            tail_linear(2)
            gate_attention(B - 1)
            tail_tanh(2)
            gate_experts(B - 2)
            act.wait_ge(s["tail_up3"], LATE)
            norm_2(B - 1, xin)
            router_exp(B - 1)
            tail_linear(LATE)
            tail_linear(LATE + 1)
            for n in range(LATE, len(TAIL)):
                tail_tanh(n)
                if n == LATE:
                    act.wait_ge(s["tail_gate"], LATE)
                    route_rows(B - 1)
                if n + 2 < len(TAIL):
                    tail_linear(n + 2)
            gate_experts(B - 1)

        @block.tensor
        def _(pe):
            def four_transposes(dst, src):
                for q in range(NQ):
                    ins = pe.transpose(dst[:, P * q:P * q + P], src[:, q, :] if len(src.shape) == 3
                                       else src[:, P * q:P * q + P], ident[:, :])
                return ins

            def scores(b, h):
                g, st = h // STEPS, h % STEPS
                G = NG * b + g
                H = STEPS * G + st
                if st == 0:
                    for p in range(2):
                        pe.wait_ge(stacked[2 * g + p], 64 * (b + 1))
                    pe.wait_ge(s["spread"], 4 * (G + 1))
                for k, j in enumerate(TILES[st]):
                    n, at = KEYS[st][k], PS_AT[st][k]
                    if k < 3:
                        after(pe, s["scopied"], NC_ * (H - 1) + CHUNK_OF[k] + 1)
                    for p in range(2):
                        pe.matmul(pS[:, at:at + n], QB[:, g % 2, p, j, :], KS[:, 2 * g + p, 0:n],
                                  start=p == 0, stop=False)
                    ins = pe.matmul(pS[:, at + n - QL:at + n], identb[:, :], cmaskb[:, :], start=False, stop=True)
                    if k != 2:
                        ins.then_inc(s["scores"], 1)

            def values(b, h):
                g, st = h // STEPS, h % STEPS
                G = NG * b + g
                H = STEPS * G + st

                def transposes(i):
                    lo, hi = BLOCK_CHUNKS[st][i]
                    pe.wait_ge(s["p_done"], before(SEARCHED, G, st) + (1, 2, SEARCHED[st])[i])
                    if i == 2 and SEARCHED[st] == 3:
                        pe.wait_ge(s["e1_done"], 4 * (H + 1))
                    after(pe, s["pt_evac"], NC_ * H + i)
                    for c in range(lo, hi):
                        ins = pe.transpose(pT[:, P * (c - lo):P * (c - lo) + P], E1[:, st, P * c:P * c + P], ident[:, :])
                    ins.then_inc(s["pt_full"], 1)

                def product(k):
                    pe.wait_ge(s["pt_evac"], NC_ * H + CHUNK_OF[k] + 1)
                    if k == 0:
                        pe.wait_ge(s["v_evac"], b + 1)
                        after(pe, s["o_evac"], H)
                    for kb in range(BLOCKS[st][k]):
                        at = P * (BLOCK_AT[st][k] + kb)
                        ins = pe.matmul(pO[:, OW * k:OW * k + OW], PT[:, at:at + P], VX[:, kb, QH * g:QH * g + QH, :],
                                        start=kb == 0, stop=kb == BLOCKS[st][k] - 1)
                    return ins

                transposes(0)
                yield
                transposes(1)
                product(0)
                yield
                transposes(2)
                product(1)
                yield
                product(2)
                product(3).then_inc(s["pv_done"], 1)
                yield

            def norm_1(bb):
                pe.wait_ge(s["ln1_done"], bb + 1)
                four_transposes(F1, xn1).then_inc(s["ln1T_full"], 1)

            def next_kq(bb, k_bank, q_bank):
                pe.wait_ge(s["hT_done"], bb + 1)
                if k_bank is F0:
                    pe.wait_ge(s["setup_dve"], SETUP_DVE)
                pe.matmul(k_bank[:, :], W["wkT"][:, :], hT[:, :], start=True, stop=True).then_inc(s["k_full"], 1)
                yield
                if k_bank is q_bank:
                    pe.wait_ge(s["k_evac"], bb + 1)
                pe.matmul(q_bank[:, :], W["wqT"][:, :], hT[:, :], start=True, stop=True).then_inc(s["q_full"], 1)
                yield
                yield
                yield

            def project_v(bb):
                for q in range(NQ):
                    ins = pe.matmul(F0[:, P * q:P * q + P], hT[:, P * q:P * q + P], W["wvT"][:, :], start=True, stop=True)
                ins.then_inc(s["v_full"], 1)

            def loop_tiles(b):
                return FT * b - (LATE if isinstance(b, int) and b == B - 1 else 0)

            def outputs_transposed(b):
                pe.wait_ge(s["norm_done"], NG * (b + 1))
                after(pe, s["c_done"], loop_tiles(b))
                for slot, j in enumerate(j for step in TILES for j in step):
                    ins = pe.matmul(F1[:, QL * j:QL * j + QL], osb[:, slot, :],
                                    W["ident32"][:, :], start=True, stop=True)
                ins.then_inc(s["OT_full"], 1)

            def attention_out(b):
                pe.wait_ge(s["OT_evac"], b + 1)
                pe.matmul(F1[:, :], W["woT"][:, :], OT[:, :], start=True, stop=True).then_inc(s["wo_full"], 1)
                yield
                pe.wait_ge(s["yT_done"], b + 1)
                after(pe, s["r_done"], loop_tiles(b))
                if not (isinstance(b, int) and b == B - 1):
                    pe.wait_ge(s["v_evac"], b + 2)
                four_transposes(F0, yT).then_inc(s["att_full"], 1)
                yield
                yield
                yield

            def norm_2_and_logits(b):
                pe.wait_ge(s["ln2_done"], b + 1)
                four_transposes(F0, xn2).then_inc(s["ln2T_full"], 1)
                pe.wait_ge(s["h2T_done"], b + 1)
                if not isinstance(b, int) or b < B - 2:
                    pe.wait_ge(s["q_evac"], b + 3)
                for q in range(NQ):
                    ins = pe.matmul(F1[:, E * q:E * q + E], h2T[:, P * q:P * q + P], W["gwT"][:, :], start=True, stop=True)
                ins.then_inc(s["log_full"], 1)

            def up1(T, t):
                pe.matmul(F0[:, :], W["w1"][:, P * t:P * t + P], h2T[:, :], start=True, stop=True)\
                    .then_inc(s["up1_full"], 1)

            def up3(T, t):
                pe.matmul(F1[:, :], W["w3"][:, P * t:P * t + P], h2T[:, :], start=True, stop=True)\
                    .then_inc(s["up3_full"], 1)

            def gate(T, t):
                pe.matmul(F0[:, :], selb[:, P * t:P * t + P], rwTb[:, :], start=True, stop=True)\
                    .then_inc(s["gate_full"], 1)

            def down(T, t, b):
                pe.wait_ge(s["h_done"], T + 1)
                if t == 0:
                    after(pe, s["fin_done"], b)
                pe.matmul(pY[:, :], W["w2"][:, P * t:P * t + P], fh[:, t % 2, :], start=t == 0, stop=False)\
                    .then_inc(s["w2_done"], 1)

            def expert_tile(b, t):
                T = FT * b + t
                if t:
                    pe.wait_ge(s["a_done"], T)
                if t > 1:
                    if t == 2:
                        pe.wait_ge(s["r_done"], T - 1)
                    gate(T - 1, t - 1)
                    down(T - 2, t - 2, b)
                if t != 1:
                    yield
                if t < FT:
                    if t > 1:
                        pe.wait_ge(s["r_done"], T)
                    up1(T, t)
                yield
                if t < FT:
                    if t:
                        pe.wait_ge(s["c_done"], T)
                    else:
                        pe.wait_ge(s["rsub_done"], b + 1)
                    up3(T, t)
                yield
                if t == 1:
                    pe.wait_ge(s["rsplit"], 6 * (b + 1))
                    pe.wait_ge(s["a_done"], T + 1)
                    four_transposes(F0, rw).then_inc(s["rwT_full"], 1)
                    yield
                    pe.wait_ge(s["rwT_done"], b + 1)
                    gate(T - 1, t - 1)
                yield

            def biases(b):
                pe.matmul(pY[:, :], W["b2"][WHOLE:WHOLE + E + 1, :], rwT[WHOLE:WHOLE + E + 1, :], start=False, stop=True).then_inc(s["y_full"], 1)

            def experts_out(b):
                yield
                pe.wait_ge(s["z_done"], b + 1)
                four_transposes(pY, zT).then_inc(s["zT_full"], 1)
                yield
                yield
                yield

            def batch(b, prep, ffn, old):
                for h in range(NH):
                    t = h - FIRST_FFN
                    if h < NH - 2:
                        scores(b, h + 2)
                    elif prep:
                        scores(b + 1, h + 2 - NH)
                    if ffn and h == 3:
                        outputs_transposed(b - 1)
                    if prep and h == 4:
                        if ffn:
                            pe.wait_ge(s["yT_done"], b)
                        norm_1(b + 1)
                    if old and h == 4:
                        down(FT * (b - 1) - 1, FT - 1, b - 2)
                        biases(b - 2)
                    beside = []
                    if old and h <= LATE:
                        if h == 1:
                            pe.wait_ge(s["v_evac"], b + 1)
                        beside.append(expert_tile(b - 2, FT - LATE + h))
                    if ffn and h == 3:
                        beside.append(attention_out(b - 1))
                    if old and h == 4:
                        beside.append(experts_out(b - 2))
                    if prep and h == 4:
                        beside.append(next_kq(b + 1, F1, F1))
                    if ffn and h >= FIRST_FFN:
                        beside.append(expert_tile(b - 1, h - FIRST_FFN))
                    if h or ffn:
                        beside.insert(0 if h in VALUES_FIRST else len(beside),
                                      values(b, h - 1) if h else values(b - 1, NH - 1))
                        run(*beside)
                    if ffn and h == 5:
                        norm_2_and_logits(b - 1)
                    if h == 0:
                        if old:
                            pe.wait_ge(s["a_done"], FT * (b - 1) - LATE + 1)
                        else:
                            pe.wait_ge(s["k_evac"], b + 1)
                        project_v(b)

            pe.wait_ge(s["w_loaded"], n_attn_loads)
            pe.wait_ge(s["setup_dve"], 2)
            for m in range(6):
                pe.matmul(F0[:, B * m:B * m + B], W["wmod"][:, D * m:D * m + D], c_silu[:, :], start=True, stop=True)
            pe.matmul(F0[:, 6 * B:6 * B + 1], W["woT"][:, :], W["bv"][:, :], start=True, stop=True)\
                .then_inc(s["setup_pe"], 1)
            norm_1(0)
            run(next_kq(0, F0, F1))
            pe.wait_ge(s["const_ready"], 7)
            scores(0, 0)
            scores(0, 1)
            batch(0, True, False, False)
            pe.wait_ge(s["ffn_loaded"], n_ffn_loads)
            pe.wait_ge(s["sel_ready"], 1)
            batch(1, True, True, False)
            with pe.Fori(2, B - 1) as b:
                batch(b, True, True, True)
            batch(B - 1, False, True, True)

            def tail_up(n):
                after(pe, s["tail_a"], n - 1)
                after(pe, s["tail_u"], n - 1)
                t = TAIL[n][1]
                pe.matmul(up1_bank[n % 2], W["w1"][:, P * t:P * t + P], h2T[:, :], start=True, stop=True)\
                    .then_inc(s["tail_up1"], 1)
                pe.matmul(up3_bank[n % 2], W["w3"][:, P * t:P * t + P], h2T[:, :], start=True, stop=True)\
                    .then_inc(s["tail_up3"], 1)

            def tail_gate(n):
                after(pe, s["tail_h"], n)
                t = TAIL[n][1]
                pe.matmul(pO[:, :], selb[:, P * t:P * t + P], rwTb[:, :], start=True, stop=True)\
                    .then_inc(s["tail_gate"], 1)

            def tail_down(n):
                pe.wait_ge(s["tail_h"], n + 1)
                b, t = TAIL[n]
                if t == 0:
                    pe.wait_ge(s["fin_done"], b)
                pe.matmul(pY[:, :], W["w2"][:, P * t:P * t + P], fh[:, n % 2, :], start=t == 0, stop=False)\
                    .then_inc(s["tail_down"], 1)

            T = FT * (B - 1) - LATE - 1
            pe.wait_ge(s["a_done"], T + 1)
            gate(T, FT - LATE - 1)
            down(T - 1, FT - LATE - 2, B - 2)
            run(values(B - 1, NH - 1))
            pe.wait_ge(s["scopied"], NC_ * NH * B)
            tail_up(0)
            pe.wait_ge(s["pt_evac"], NC_ * NH * B)
            tail_up(1)
            pe.wait_ge(s["o_evac"], NH * B)
            tail_gate(0)
            down(T, FT - LATE - 1, B - 2)
            outputs_transposed(B - 1)
            tail_down(0)
            tail_gate(1)
            attention = attention_out(B - 1)
            next(attention)
            tail_up(2)
            tail_down(1)
            tail_gate(2)
            next(attention)
            tail_down(2)
            biases(B - 2)
            norm_2_and_logits(B - 1)
            run(experts_out(B - 2))
            tail_up(LATE)
            tail_up(LATE + 1)
            pe.wait_ge(s["rsplit"], 6 * B)
            four_transposes(F0, rw).then_inc(s["rwT_full"], 1)
            pe.wait_ge(s["rwT_done"], B)
            for n in range(LATE, len(TAIL)):
                tail_gate(n)
                if n + 2 < len(TAIL):
                    tail_up(n + 2)
                tail_down(n)
            biases(B - 1)
            run(experts_out(B - 1))


SETUP_DVE = 17


def kernel(**inputs):
    import numpy as np
    import concourse.bacc as bacc
    from concourse.bass_utils import run_bass_kernel_spmd as run

    a = {k: np.asarray(v) for k, v in inputs.items()}

    def col(v):
        return v.reshape(P, 1)

    def hidden(w, sw):
        w = np.concatenate([w, sw[None]], 0).transpose(1, 0, 2).reshape(D, (E + 1) * HID)
        return np.pad(w, ((0, 0), (0, FT * P - w.shape[1])))

    def hidden_col(bv, sbv):
        v = np.concatenate([bv, sbv[None]], 0).reshape(-1)
        return np.pad(v, (0, FT * P - v.size)).reshape(FT, P).T

    w2 = np.concatenate([a["L0_ffn_w2"], a["L0_ffn_sw2"][None]], 0).reshape((E + 1) * HID, D)
    w2 = np.pad(w2, ((0, FT * P - w2.shape[0]), (0, 0))).reshape(FT, P, D).transpose(1, 0, 2).reshape(P, FT * D)
    sel = np.zeros((E + 1, FT * P), np.float32)
    for e in range(E + 1):
        sel[e, e * HID:(e + 1) * HID] = 0.5
    b2 = np.concatenate([a["L0_ffn_b2"], a["L0_ffn_sb2"][None]], 0)
    w = {
        "cT": a["L0_c"].T, "wmod": a["L0_wmod"], "ident": np.eye(P, dtype=np.float32),
        "cmask": np.tile(np.triu(np.full((QL, QL), MASKED, np.float32), 1), (QH, 1)),
        "rows": np.repeat(np.eye(2, dtype=np.float32), P // 2, 0), "own": np.repeat(np.eye(QH, dtype=np.float32), QL, 0),
        "ident32": np.tile(np.eye(QL, dtype=np.float32), (QH, 1)),
        "wqT": a["L0_attn_Wq"].T, "wkT": a["L0_attn_Wk"].T, "wvT": a["L0_attn_Wv"].T, "woT": a["L0_attn_Wo"].T,
        "bq": col(a["L0_attn_bq"]), "bk": col(a["L0_attn_bk"]), "bv": col(a["L0_attn_bv"]), "bo": col(a["L0_attn_bo"]),
        "gwT": a["L0_ffn_gate_w"].T, "gb": np.tile(a["L0_ffn_gate_b"][None], (P, 1)),
        "iota": np.tile(np.arange(E, dtype=np.float32)[None], (P, 1)),
        "w1": hidden(a["L0_ffn_w1"], a["L0_ffn_sw1"]), "w3": hidden(a["L0_ffn_w3"], a["L0_ffn_sw3"]), "w2": w2,
        "b1": hidden_col(a["L0_ffn_b1"], a["L0_ffn_sb1"]), "b3": hidden_col(a["L0_ffn_b3"], a["L0_ffn_sb3"]),
        "b2": np.pad(b2, ((WHOLE, 0), (0, 0))), "sel": np.tile(sel, (3, 1)),
    }
    nc = bacc.Bacc("TRN2", target_bir_lowering=False, num_devices=1)
    arrays = {"in_x": np.ascontiguousarray(a["L0_attn_x"])}
    x_d = nc.dram_tensor("in_x", [B, N, D], F32, kind="ExternalInput").ap()
    w_d = {}
    for name, v in w.items():
        arrays["in_" + name] = np.ascontiguousarray(v)
        w_d[name] = nc.dram_tensor("in_" + name, list(v.shape), F32, kind="ExternalInput").ap()
    out_d = nc.dram_tensor("out", [B, N, D], F32, kind="ExternalOutput").ap()
    parts_d = nc.dram_tensor("parts", [2, PAIRS, P, N], BF16, kind="Internal").ap()
    build_program(nc, x_d, w_d, parts_d, out_d)
    r = run(nc, [arrays], core_ids=[0])
    return r.results[0]["out"]
```
